# Optimizing a Trainium2 kernel written in Bass

```python
import numpy as np
import jax
import jax.numpy as jnp

def _softmax(x, axis=-1):
    return jax.nn.softmax(x, axis=axis)

def _gelu(x):
    return jax.nn.gelu(x, approximate=True)

def _silu(x):
    return jax.nn.silu(x)

def _sigmoid(x):
    return jax.nn.sigmoid(x)

def _layernorm(x, axis=-1, eps=1e-05):
    m = jnp.mean(x, axis=axis, keepdims=True)
    v = jnp.var(x, axis=axis, keepdims=True)
    return (x - m) / jnp.sqrt(v + eps)

def _scatter_add(tgt, idx, src, axis=0):
    return tgt.at[idx].add(src)

def _segment_sum(src, seg, n):
    return jax.ops.segment_sum(src, seg, n)
kernel_name = 'mk_seq_postln_d1_jaxref_r8_9eb48a'

def setup_inputs(seed: int=0):
    np.random.seed(seed)
    _w = jnp.asarray

    def _L0_attn_setup():
        import jax, jax.numpy as jnp
        import numpy as np
        H = 32
        D = 64
        BS = 32
        LAYER_IDX = 0
        NUM_LAYERS = 32
        EPS = 1e-05

        def _decay_buffers():
            base = 1.0 / 2.0 ** (8.0 / H)
            rate = base ** (jnp.arange(H, dtype=jnp.float32) + 1.0)
            factor = 1.0 - LAYER_IDX / (NUM_LAYERS - 1 + 1e-05) + 1e-05
            slope = (rate * factor)[:, None, None]
            r = jnp.arange(BS, dtype=jnp.float32) + 1.0
            query_decay = jnp.exp(-slope * r[:, None])
            key_decay = jnp.exp(-slope * (BS - r[:, None]))
            dd = r[:, None] - r[None, :]
            dd = slope * dd[None, :, :]
            dd = jnp.where(dd >= 0, -dd, -jnp.inf)
            diagonal_decay = jnp.exp(dd)[None]
            block_decay = jnp.exp(-slope * BS)
            return (slope, query_decay, key_decay, diagonal_decay, block_decay)

        def _rmsnorm(x, w):
            v = jnp.mean(x.astype(jnp.float32) ** 2, axis=-1, keepdims=True)
            return (x * jax.lax.rsqrt(v + EPS)).astype(x.dtype) * w
        key = jax.random.key(seed)
        ks = jax.random.split(key, 4)
        b, s, hid = (2, 512, 256)
        return {'hidden_states': jax.random.normal(ks[0], (b, s, hid), jnp.float32), 'qkv_w': jax.random.normal(ks[1], (3 * H * D, hid), jnp.float32) * 0.02, 'out_w': jax.random.normal(ks[2], (hid, H * D), jnp.float32) * 0.02, 'gate_w': jax.random.normal(ks[3], (H * D, hid), jnp.float32) * 0.02, 'norm_w': jnp.ones((H * D,), jnp.float32)}
    _L0_attn_in = _L0_attn_setup()

    def _L0_ffn_setup():
        import jax, jax.numpy as jnp
        import numpy as np
        E, K, H, F = (64, 6, 256, 96)
        G, KG = (8, 4)
        SHARED_F = 96
        SCALE = 2.5
        T = 2 * 128
        CAP = 2 * (T * K // E)

        def _grouped_topk(logits, bias):
            scores = jax.nn.sigmoid(logits.astype(jnp.float32))
            scores_b = scores + bias[None, :]
            gs = scores_b.reshape(-1, G, E // G)
            group_scores = jnp.sum(jax.lax.top_k(gs, 2)[0], axis=-1)
            gidx = jax.lax.top_k(group_scores, KG)[1]
            rows = jnp.arange(group_scores.shape[0])[:, None]
            group_mask = jnp.zeros_like(group_scores).at[rows, gidx].set(1.0)
            score_mask = jnp.repeat(group_mask, E // G, axis=-1) > 0
            tmp = jnp.where(score_mask, scores_b, -jnp.inf)
            topk_ids = jax.lax.top_k(tmp, K)[1]
            topk_w = jnp.take_along_axis(scores, topk_ids, axis=-1)
            topk_w = topk_w / jnp.sum(topk_w, axis=-1, keepdims=True)
            return (topk_w * SCALE, topk_ids)

        def _routed_moe(x, topk_w, topk_ids, w_gate, w_up, w_down):
            Tn = x.shape[0]
            flat_e = topk_ids.reshape(-1)
            order = jnp.argsort(flat_e)
            se = flat_e[order]
            pos = jnp.arange(Tn * K) - jnp.searchsorted(se, se, side='left')
            tok = order // K
            valid = pos < CAP
            slot = jnp.where(valid, pos, CAP)
            buf = jnp.zeros((E, CAP + 1, H), x.dtype).at[se, slot].set(x[tok])[:, :CAP]
            h = jax.nn.silu(jnp.einsum('ech,ehf->ecf', buf, w_gate)) * jnp.einsum('ech,ehf->ecf', buf, w_up)
            out = jnp.einsum('ecf,efh->ech', h, w_down)
            gathered = out[se, jnp.minimum(pos, CAP - 1)] * valid.astype(x.dtype)[:, None]
            w = topk_w.reshape(-1)[order].astype(x.dtype)[:, None]
            return jax.ops.segment_sum(gathered * w, tok, num_segments=Tn)
        key = jax.random.key(seed)
        ks = jax.random.split(key, 9)
        s = 0.02
        return dict(hidden_states=jax.random.normal(ks[0], (2, 128, H), jnp.float32), gate_w=jax.random.normal(ks[1], (H, E), jnp.float32) * s, bias=jax.random.normal(ks[2], (E,), jnp.float32) * s, w_gate=jax.random.normal(ks[3], (E, H, F), jnp.float32) * s, w_up=jax.random.normal(ks[4], (E, H, F), jnp.float32) * s, w_down=jax.random.normal(ks[5], (E, F, H), jnp.float32) * s, ws_gate=jax.random.normal(ks[6], (H, SHARED_F), jnp.float32) * s, ws_up=jax.random.normal(ks[7], (H, SHARED_F), jnp.float32) * s, ws_down=jax.random.normal(ks[8], (SHARED_F, H), jnp.float32) * s)
    _L0_ffn_in = _L0_ffn_setup()
    _d = {'L0_attn_hidden_states': _L0_attn_in['hidden_states'], 'L0_attn_qkv_w': _L0_attn_in['qkv_w'], 'L0_attn_out_w': _L0_attn_in['out_w'], 'L0_attn_gate_w': _L0_attn_in['gate_w'], 'L0_attn_norm_w': _L0_attn_in['norm_w'], 'L0_ffn_gate_w': _L0_ffn_in['gate_w'], 'L0_ffn_bias': _L0_ffn_in['bias'], 'L0_ffn_w_gate': _L0_ffn_in['w_gate'], 'L0_ffn_w_up': _L0_ffn_in['w_up'], 'L0_ffn_w_down': _L0_ffn_in['w_down'], 'L0_ffn_ws_gate': _L0_ffn_in['ws_gate'], 'L0_ffn_ws_up': _L0_ffn_in['ws_up'], 'L0_ffn_ws_down': _L0_ffn_in['ws_down']}
    _x0 = _d['L0_attn_hidden_states']
    _d['L0_attn_hidden_states'] = jax.random.normal(jax.random.fold_in(jax.random.key(seed), 1), (16, 256, 256), dtype=_x0.dtype)
    del _x0
    return _d

def reference(L0_attn_hidden_states, L0_attn_qkv_w, L0_attn_out_w, L0_attn_gate_w, L0_attn_norm_w, L0_ffn_gate_w, L0_ffn_bias, L0_ffn_w_gate, L0_ffn_w_up, L0_ffn_w_down, L0_ffn_ws_gate, L0_ffn_ws_up, L0_ffn_ws_down):

    def _L0_attn_ref(hidden_states, qkv_w, out_w, gate_w, norm_w):
        import jax, jax.numpy as jnp
        import numpy as np
        H = 32
        D = 64
        BS = 32
        LAYER_IDX = 0
        NUM_LAYERS = 32
        EPS = 1e-05

        def _decay_buffers():
            base = 1.0 / 2.0 ** (8.0 / H)
            rate = base ** (jnp.arange(H, dtype=jnp.float32) + 1.0)
            factor = 1.0 - LAYER_IDX / (NUM_LAYERS - 1 + 1e-05) + 1e-05
            slope = (rate * factor)[:, None, None]
            r = jnp.arange(BS, dtype=jnp.float32) + 1.0
            query_decay = jnp.exp(-slope * r[:, None])
            key_decay = jnp.exp(-slope * (BS - r[:, None]))
            dd = r[:, None] - r[None, :]
            dd = slope * dd[None, :, :]
            dd = jnp.where(dd >= 0, -dd, -jnp.inf)
            diagonal_decay = jnp.exp(dd)[None]
            block_decay = jnp.exp(-slope * BS)
            return (slope, query_decay, key_decay, diagonal_decay, block_decay)

        def _rmsnorm(x, w):
            v = jnp.mean(x.astype(jnp.float32) ** 2, axis=-1, keepdims=True)
            return (x * jax.lax.rsqrt(v + EPS)).astype(x.dtype) * w
        b, s, hid = hidden_states.shape
        nb = s // BS
        _, qd, kd, dd, bd = _decay_buffers()
        qkv = jax.nn.silu(hidden_states @ qkv_w.T)
        qkv = qkv.reshape(b, s, H, 3 * D)
        q, k, v = jnp.split(qkv, 3, axis=-1)

        def to_blocks(t):
            return t.transpose(0, 2, 1, 3).reshape(b, H, nb, BS, D).transpose(2, 0, 1, 3, 4)
        qb, kb, vb = (to_blocks(q), to_blocks(k), to_blocks(v))
        qd_ = qd[None]
        kd_ = kd[None]
        bd_ = bd[None]

        def step(state, blk):
            qi, ki, vi = blk
            aw = jnp.einsum('bhid,bhjd->bhij', qi, ki) * dd
            intra = jnp.einsum('bhij,bhjd->bhid', aw, vi)
            inter = jnp.einsum('bhid,bhde->bhie', qi * qd_, state)
            new_state = state * bd_ + jnp.einsum('bhsd,bhse->bhde', ki * kd_, vi)
            return (new_state, intra + inter)
        state0 = jnp.zeros((b, H, D, D), hidden_states.dtype)
        _, ys = jax.lax.scan(step, state0, (qb, kb, vb))
        attn = ys.transpose(1, 2, 0, 3, 4).reshape(b, H, s, D)
        attn = attn.transpose(0, 2, 1, 3).reshape(b, s, H * D)
        attn = _rmsnorm(attn, norm_w)
        gate = jax.nn.sigmoid(hidden_states @ gate_w.T)
        return gate * attn @ out_w.T

    def _L0_ffn_ref(hidden_states, gate_w, bias, w_gate, w_up, w_down, ws_gate, ws_up, ws_down):
        import jax, jax.numpy as jnp
        import numpy as np
        E, K, H, F = (64, 6, 256, 96)
        G, KG = (8, 4)
        SHARED_F = 96
        SCALE = 2.5
        T = 2 * 128
        CAP = 2 * (T * K // E)

        def _grouped_topk(logits, bias):
            scores = jax.nn.sigmoid(logits.astype(jnp.float32))
            scores_b = scores + bias[None, :]
            gs = scores_b.reshape(-1, G, E // G)
            group_scores = jnp.sum(jax.lax.top_k(gs, 2)[0], axis=-1)
            gidx = jax.lax.top_k(group_scores, KG)[1]
            rows = jnp.arange(group_scores.shape[0])[:, None]
            group_mask = jnp.zeros_like(group_scores).at[rows, gidx].set(1.0)
            score_mask = jnp.repeat(group_mask, E // G, axis=-1) > 0
            tmp = jnp.where(score_mask, scores_b, -jnp.inf)
            topk_ids = jax.lax.top_k(tmp, K)[1]
            topk_w = jnp.take_along_axis(scores, topk_ids, axis=-1)
            topk_w = topk_w / jnp.sum(topk_w, axis=-1, keepdims=True)
            return (topk_w * SCALE, topk_ids)

        def _routed_moe(x, topk_w, topk_ids, w_gate, w_up, w_down):
            Tn = x.shape[0]
            flat_e = topk_ids.reshape(-1)
            order = jnp.argsort(flat_e)
            se = flat_e[order]
            pos = jnp.arange(Tn * K) - jnp.searchsorted(se, se, side='left')
            tok = order // K
            valid = pos < CAP
            slot = jnp.where(valid, pos, CAP)
            buf = jnp.zeros((E, CAP + 1, H), x.dtype).at[se, slot].set(x[tok])[:, :CAP]
            h = jax.nn.silu(jnp.einsum('ech,ehf->ecf', buf, w_gate)) * jnp.einsum('ech,ehf->ecf', buf, w_up)
            out = jnp.einsum('ecf,efh->ech', h, w_down)
            gathered = out[se, jnp.minimum(pos, CAP - 1)] * valid.astype(x.dtype)[:, None]
            w = topk_w.reshape(-1)[order].astype(x.dtype)[:, None]
            return jax.ops.segment_sum(gathered * w, tok, num_segments=Tn)
        orig_shape = hidden_states.shape
        x = hidden_states.reshape(-1, H)
        router_logits = x @ gate_w
        topk_w, topk_ids = _grouped_topk(router_logits, bias)
        y = _routed_moe(x, topk_w, topk_ids, w_gate, w_up, w_down)
        shared = jax.nn.silu(x @ ws_gate) * (x @ ws_up) @ ws_down
        return (y + shared).reshape(orig_shape)
    x = L0_attn_hidden_states
    x = _layernorm(x + _L0_attn_ref(x, L0_attn_qkv_w, L0_attn_out_w, L0_attn_gate_w, L0_attn_norm_w), axis=-1)
    x = _layernorm(x + _L0_ffn_ref(x, L0_ffn_gate_w, L0_ffn_bias, L0_ffn_w_gate, L0_ffn_w_up, L0_ffn_w_down, L0_ffn_ws_gate, L0_ffn_ws_up, L0_ffn_ws_down), axis=-1)
    return x

_drawn_inputs = setup_inputs


def setup_inputs(seed=0):
    import zlib

    import numpy as np

    out = dict(_drawn_inputs(seed))
    spreads = {'L0_attn_norm_w': (1.0, 0.2)}
    factors = {'L0_ffn_gate_w': 8.0,
     'L0_ffn_bias': 8.0,
     'L0_ffn_w_gate': 8.0,
     'L0_ffn_w_up': 8.0,
     'L0_ffn_w_down': 8.0,
     'L0_ffn_ws_gate': 5.553,
     'L0_ffn_ws_up': 5.493,
     'L0_ffn_ws_down': 5.476}
    for name, (base, spread) in spreads.items():
        noise = np.random.default_rng([zlib.crc32(name.encode()), seed]).standard_normal(out[name].shape)
        drawn = base * np.exp(spread * noise) if base else spread * noise
        out[name] = jnp.asarray(drawn.astype(out[name].dtype))
    for name, factor in factors.items():
        out[name] = (out[name] * factor).astype(out[name].dtype)
    return out
```

```python
import concourse.bass as bass
from concourse import mybir
from contextlib import ExitStack

F32 = mybir.dt.float32
F16 = mybir.dt.float16
U32 = mybir.dt.uint32
ALU = mybir.AluOpType
ACT = mybir.ActivationFunctionType

P = 128
SEQS, T, HID = 16, 256, 256
TOK = SEQS * T
HEADS, HD = 32, 64
INNER = HEADS * HD
QH = 4
NQ = HEADS // QH
STEPS = SEQS * NQ
NT = T // P
NC = HID // P
QW, GW, OW = NC * 3 * 256, NC * 256, 2 * HID
PREP = QW + GW + OW
W_SCALE = 1024.0
EPS = 1e-5
EXP, TOPK, GROUPS, TOPG, FF = 64, 6, 8, 4, 96
CAP = 2 * ((2 * 128) * TOPK // EXP)
ROUTE_SCALE = 2.5
PAIRS = EXP // 2
ROW = HID + EXP
BANDS = 112
DUMMY = 64
NEG = -1e30
FAR = 8192.0
RING = 4
PAIR_W = 2 * 2 * NC * FF + 2 * HID
FIN = 4
LN1_LINKS, ROUTE_LINKS, FIND_LINKS, FIN_LINKS = 3, 14, 5, 3


def wait(eng, sem, value):
    if not (isinstance(value, int) and value <= 0):
        eng.wait_ge(sem, value)


def wait_apart(eng, passed, *waits):
    for sem, v in waits:
        wait(eng, sem, v)
    eng.sem_inc(passed, 1)


class Chain:

    def __init__(self, eng, sem, before, passed=None):
        self.eng, self.sem, self.before, self.n, self.passed = eng, sem, before, 0, passed

    def link(self, instruction):
        self.n += 1
        instruction.then_inc(self.sem, 1)
        if self.passed is None:
            self.eng.wait_ge(self.sem, self.before + self.n)
        else:
            wait_apart(self.eng, self.passed, (self.sem, self.before + self.n))


def block_kernel(nc, x, xT, wprep, normw, decay, eye, tri, w_router, bias2, w_shared, w_shared_down,
                 w_experts, w_down, pair_pick, out):
    grows = nc.dram_tensor("gather_rows", (TOK, ROW), F32, kind="Internal").ap()
    sums = [nc.dram_tensor(f"sums{i}", (TOK + DUMMY, HID), F32, kind="Internal").ap() for i in range(2)]
    x_t = x.rearrange("(b t p) n -> b p t n", t=NT, p=P)
    xT_t = xT.rearrange("(c p) (b n) -> b p c n", p=P, b=SEQS)
    rows_t = grows.rearrange("(b t p) n -> b p t n", t=NT, p=P)
    base_t = sums[0][0:TOK, :].rearrange("(b t p) n -> b p t n", t=NT, p=P)

    with ExitStack() as ctx:
        def sb(name, shape, dt=F32):
            return ctx.enter_context(nc.sbuf_tensor(f"sb_{name}", shape, dt))

        def sem(name):
            return ctx.enter_context(nc.semaphore(name))

        W = sb("W", [P, 2 * NQ * (QW + GW)], F16)
        Wv = W[:, :].rearrange("p (s q n) -> p s q n", s=2, q=NQ)
        Wo = sb("Wo", [P, 2, NQ, OW], F16)
        stage = sb("stage", [P, 2, PREP])
        D = sb("D", [P, NQ, QH * T])
        nw = sb("nw", [P, HEADS // 2])
        xs = sb("xs", [P, NC * T])
        xh = sb("xh", [P, 2 * NC * T], F16)
        xl = sb("xl", [P, 2 * NC * T], F16)
        xn = sb("xn", [P, NT, HID])
        q32 = sb("q32", [P, 2, T])
        k32 = sb("k32", [P, 2, T])
        q2h = [sb(f"q2h{i}", [P, 2, 2, T], F16) for i in range(2)]
        q2l = [sb(f"q2l{i}", [P, 2, 2, T], F16) for i in range(2)]
        k2 = [sb(f"k2{i}", [P, 2, 2, T], F16) for i in range(2)]
        khB = sb("khB", [P, 2, T], F16)
        v32 = [sb(f"v32{i}", [P, NT, QH * HD]) for i in range(2)]
        gt = [sb(f"gt{i}", [P, 2 * T]) for i in range(2)]
        S = sb("S", [P, QH, T + P])
        y32 = sb("y32", [P, 2 * T])
        yh = sb("yh", [P, 2 * T], F16)
        yl = sb("yl", [P, 2 * T], F16)
        sq = sb("sq", [P, 2 * T])
        acc = sb("acc", [P, 2 * T])
        o32 = sb("o32", [P, NT, HID])
        z = sb("z", [P, NT, HID])
        ssv = sb("ssv", [P, NT])
        rstd1 = sb("rstd1", [P, NT])
        mhalf = sb("mhalf", [P, FIN])
        st6 = sb("st6", [P, FIN, 6])
        mv = sb("mv", [P, FIN, 2])
        vv = sb("vv", [P, FIN])
        rstd2 = sb("rstd2", [P, FIN])
        nmr = sb("nmr", [P, 2, FIN])
        frs = sb("frs", [P, 2, FIN])
        fmv = sb("fmv", [P, 2, FIN, 2])
        xr = sb("xr", [P, NT, ROW])
        x1T = sb("x1T", [P, NC, T])
        wr = sb("wr", [P, NC, EXP])
        wsh = sb("wsh", [P, NC, 2 * FF])
        wsd = sb("wsd", [FF, HID])
        b2 = sb("b2", [P, NT, EXP])
        ident = sb("ident", [P, P])
        triu = sb("triu", [P, T], F16)
        triu32 = sb("triu32", [P, T])
        ones = sb("ones", [P, 1])
        th = sb("th", [P, NT, EXP])
        sc = sb("sc", [P, NT, EXP])
        scb = sb("scb", [P, NT, EXP])
        top = sb("top", [P, NT * GROUPS, 8])
        gs = sb("gs", [P, NT, 2 * GROUPS])
        g8 = sb("g8", [P, NT, 8])
        grep = sb("grep", [P, NT, 2 * GROUPS])
        uns = sb("uns", [P, NT, GROUPS])
        masked = sb("masked", [P, NT, EXP])
        t8 = sb("t8", [P, NT, 8])
        mrep = sb("mrep", [P, NT, EXP])
        mask = sb("mask", [P, NT, EXP], F16)
        wsel = sb("wsel", [P, NT, EXP])
        wsum = sb("wsum", [P, NT])
        wrec = sb("wrec", [P, NT])
        hs = sb("hs", [FF, T])
        hT = sb("hT", [FF, T])
        bs = sb("bs", [P, NT, HID])
        cumb = sb("cumb", [EXP, T + CAP])
        carry = sb("carry", [EXP, 1])
        vals = sb("vals", [EXP, CAP])
        found = sb("found", [EXP, CAP], U32)
        foundf = sb("foundf", [EXP, CAP])
        pen = sb("pen", [EXP, CAP])
        cand = sb("cand", [EXP, CAP])
        ids = sb("ids", [EXP, CAP])
        idsg = sb("idsg", [EXP, CAP])
        first = sb("first", [EXP, 1])
        dummy = sb("dummy", [EXP, CAP])
        pick = sb("pick", [EXP, 2 + PAIRS])
        bands = sb("bands", [EXP, BANDS])
        gidx = sb("gidx", [BANDS, PAIRS], U32)
        sidx = sb("sidx", [CAP, EXP], U32)
        gcol = sb("gcol", [BANDS, 4], U32)
        scol = sb("scol", [CAP, 4, 2], U32)
        zeros = sb("zeros", [P, 512])
        flat = stage[:, :, :].rearrange("p s n -> p (s n)")
        xg = flat[0:BANDS, 0:4 * ROW].rearrange("p (s n) -> p s n", s=4)
        wo = flat[0:CAP, 1280:2304].rearrange("p (s e n) -> p s e n", s=2, e=2)
        xgT = flat[:, 2304:2752].rearrange("p (s c n) -> p s c n", s=2, c=NC)
        mhs = flat[0:FF, 2752:2944].rearrange("p (s n) -> p s n", s=2)
        mh = flat[0:FF, 2944:3136].rearrange("p (s n) -> p s n", s=2)
        W32 = W[:, :].bitcast(F32)
        ring = [W32[:, r * PAIR_W:(r + 1) * PAIR_W] for r in range(RING)]
        ring_gu = [s[:, 0:4 * NC * FF].rearrange("p (e g c f) -> p e g c f", e=2, g=2, c=NC) for s in ring]
        ring_d = [s[0:FF, 4 * NC * FF:PAIR_W].rearrange("p (e n) -> p e n", e=2) for s in ring]
        D1 = D[:, :, :].rearrange("p q n -> p (q n)")
        f0 = [D1[:, r * 1024:(r + 1) * 1024].rearrange("p (k n) -> p k n", k=FIN) for r in range(4)]
        f1 = [D1[:, (4 + r) * 1024:(5 + r) * 1024].rearrange("p (k n) -> p k n", k=FIN) for r in range(4)]

        pQ, pK, pV, pG, pS0, pS1, pC, pO = [
            ctx.enter_context(nc.psum_tensor(n, [P, 512], F32))
            for n in ("pQ", "pK", "pV", "pG", "pS0", "pS1", "pC", "pO")]
        pT, pH, pDn = [pQ, pG], [pK, pS0], [pV, pS1]

        s_dve_passed, s_pool_passed = sem("s_dve_passed"), sem("s_pool_passed")
        s_const = sem("s_const")
        s_init = sem("s_init")
        s_tri = sem("s_tri")
        s_nw = sem("s_nw")
        s_mhalf = sem("s_mhalf")
        s_stage = [sem(f"s_stage{i}") for i in range(2)]
        s_wh = sem("s_wh")
        s_wl = sem("s_wl")
        s_xin = sem("s_xin")
        s_xh = sem("s_xh")
        s_x = sem("s_x")
        s_xn = sem("s_xn")
        s_q, s_k, s_v, s_g = sem("s_q"), sem("s_k"), sem("s_v"), sem("s_g")
        s_qe, s_ke, s_ve, s_ge = sem("s_qe"), sem("s_ke"), sem("s_ve"), sem("s_ge")
        s_ql = sem("s_ql")
        s_q2 = sem("s_q2")
        s_k2 = sem("s_k2")
        s_S = sem("s_S")
        s_Sm = sem("s_Sm")
        s_C = sem("s_C")
        s_y = sem("s_y")
        s_yh, s_yl = sem("s_yh"), sem("s_yl")
        s_sq = sem("s_sq")
        s_acc = sem("s_acc")
        s_D = sem("s_D")
        s_oe = sem("s_oe")
        s_ss, s_sse = sem("s_ss"), sem("s_sse")
        s_rstd1 = sem("s_rstd1")
        s_ln1 = sem("s_ln1")
        s_z = sem("s_z")
        s_var, s_rstd2 = sem("s_var"), sem("s_rstd2")
        s_x1 = sem("s_x1")
        s_T, s_x1T = sem("s_T"), sem("s_x1T")
        s_r, s_th = sem("s_r"), sem("s_th")
        s_route = sem("s_route")
        s_mask, s_w = sem("s_mask"), sem("s_w")
        s_gu, s_hs, s_h = sem("s_gu"), sem("s_hs"), sem("s_h")
        s_dn, s_bs = sem("s_dn"), sem("s_bs")
        s_cum, s_cume = sem("s_cum"), sem("s_cume")
        s_find = sem("s_find")
        s_rows, s_base = sem("s_rows"), sem("s_base")
        s_zero = sem("s_zero")
        s_ids, s_idp, s_idx = sem("s_ids"), sem("s_idp"), sem("s_idx")
        s_slots = sem("s_slots")
        s_gcol = sem("s_gcol")
        s_ring = [sem(f"s_ring{i}") for i in range(RING)]
        s_gath = [sem(f"s_gath{i}") for i in range(4)]
        s_mT, s_xgT = sem("s_mT"), sem("s_xgT")
        s_mgu, s_mhs, s_mh = sem("s_mgu"), sem("s_mhs"), sem("s_mh")
        s_md, s_wo = sem("s_md"), sem("s_wo")
        s_sc = [sem(f"s_sc{i}") for i in range(2)]
        s_fl = [sem(f"s_fl{i}") for i in range(4)]
        s_fin = sem("s_fin")
        s_fv, s_frs, s_nm, s_fo, s_out = sem("s_fv"), sem("s_frs"), sem("s_nm"), sem("s_fo"), sem("s_out")

        block = ctx.enter_context(nc.Block())
        HALF = [(0, 64), (64, 128)]

        def has(g):
            return not isinstance(g, int) or 0 <= g < STEPS

        def sequences(eng, step):
            for q in range(NQ):
                step(0, q)
            with eng.Fori(1, SEQS) as b:
                for q in range(NQ):
                    step(b, q)
            for q in range(NQ):
                step(SEQS, q)

        def behind(b):
            return not (isinstance(b, int) and b == 0)

        @block.sync
        def _(sp):
            def load_weights(Q):
                if Q >= 2:
                    sp.wait_ge(s_wl, Q - 1)
                sp.dma_start(stage[:, Q % 2, :], wprep[Q]).then_inc(s_stage[Q % 2], 16)
                sp.dma_start(D[:, Q, :], decay[Q]).then_inc(s_stage[Q % 2], 16)

            sp.dma_start(xs[:, :].rearrange("p (c n) -> p c n", c=NC), xT_t[0]).then_inc(s_xin, 16)
            sp.dma_start(nw[:, :], normw).then_inc(s_const, 16)
            load_weights(0)
            load_weights(1)
            small = [(ident[:, :], eye), (triu32[:, :], tri), (wr[:, :, :], w_router), (b2[:, :, :], bias2),
                     (wsh[:, :, :], w_shared), (wsd[:, :], w_shared_down), (pick[:, :], pair_pick)]
            for dst, src in small:
                sp.dma_start(dst, src).then_inc(s_const, 16)
            sp.wait_ge(s_x, 1)
            sp.dma_start(xs[:, :].rearrange("p (c n) -> p c n", c=NC), xT_t[1]).then_inc(s_xin, 16)
            for Q in range(2, NQ):
                load_weights(Q)
            sp.wait_ge(s_init, 1)
            sp.dma_start(sums[1][0:TOK, :].rearrange("(p k) n -> p (k n)", p=P).rearrange("p (r m) -> p r m", m=512),
                         zeros[:, :].unsqueeze(1).broadcast_to([P, TOK * HID // P // 512, 512])).then_inc(s_zero, 16)
            for i, opened in enumerate((s_rows, s_base)):
                sp.dma_start(sums[i][TOK:TOK + DUMMY, :], zeros[0:DUMMY, 0:HID]).then_inc(opened, 16)

            def sequence(b):
                if not (isinstance(b, int) and b == SEQS):
                    sp.wait_ge(s_x, b + 1)
                    ahead = (b + 1) % SEQS
                    sp.dma_start(xs[:, :].rearrange("p (c n) -> p c n", c=NC),
                                 xT_t[bass.ds(ahead, 1)].rearrange("o p c n -> (o p) c n")).then_inc(s_xin, 16)
                sp.wait_ge(s_z, b)
                sp.dma_start(xn[:, :, :], x_t[bass.ds(b - 1, 1)].rearrange("o p t n -> (o p) t n")).then_inc(s_xn, 16)
                sp.wait_ge(s_w, b)
                sp.dma_start(rows_t[bass.ds(b - 1, 1)].rearrange("o p t n -> (o p) t n"), xr[:, :, :]).then_inc(s_rows, 16)
                sp.wait_ge(s_bs, b + 1)
                sp.dma_start(base_t[bass.ds(b - 1, 1)].rearrange("o p t n -> (o p) t n"), bs[:, :, :]).then_inc(s_base, 16)

            with sp.Fori(1, SEQS) as b:
                sequence(b)

            def load_pair(p, r):
                one = bass.ds(p, 1)
                sp.dma_start(ring[r][:, 0:4 * NC * FF], w_experts[one].rearrange("o p n -> (o p) n")).then_inc(s_ring[r], 16)
                sp.dma_start(ring[r][0:FF, 4 * NC * FF:PAIR_W], w_down[one].rearrange("o p n -> (o p) n")).then_inc(s_ring[r], 16)

            sp.wait_ge(s_g, STEPS)
            for r in range(RING):
                load_pair(r, r)
            sequence(SEQS)
            with sp.Fori(1, PAIRS // RING) as i:
                for r in range(RING):
                    sp.wait_ge(s_md, RING * (i - 1) + r + 1)
                    load_pair(RING * i + r, r)

            parts = [a[0:TOK, :].rearrange("(p c k) n -> c p k n", p=P, k=FIN) for a in (*sums, out)]
            for i in range(2):
                sp.wait_ge(s_sc[i], 16 * PAIRS)
            chunks = TOK // P // FIN
            for c in range(chunks + 3):
                if c < chunks:
                    if c >= 4:
                        sp.wait_ge(s_out, 16 * (c - 3))
                    sp.dma_start(f0[c % 4], parts[0][c]).then_inc(s_fl[c % 4], 16)
                    sp.dma_start(f1[c % 4], parts[1][c]).then_inc(s_fl[c % 4], 16)
                if c >= 3:
                    sp.wait_ge(s_fo, c - 2)
                    sp.dma_start(parts[2][c - 3], f1[(c - 3) % 4]).then_inc(s_out, 16)
            sp.wait_ge(s_out, 16 * chunks)

        @block.tensor
        def _(pe):
            def group(dst, terms, **kw):
                for i, (a, m) in enumerate(terms):
                    last = nc.tensor.matmul(dst, a, m, start=(i == 0), stop=(i == len(terms) - 1), **kw)
                return last

            PASSES = [(0, 0), (1, 0), (0, 1)]

            def tokens(b, part, c, t0, n):
                at = (b % 2) * (NC * T) + (c * T + t0)
                return (xh, xl)[part][:, bass.ds(at, n)]

            def weights(part, q, col, n):
                return Wv[:, part, q, col:col + n]

            def transposed(b, q, bank, cols):
                for u in range(2):
                    last = group(bank[:, u * T:(u + 1) * T],
                                 [(weights(w, q, cols(c) + u * P, P), tokens(b, t, c, 0, T))
                                  for c in range(NC) for w, t in PASSES])
                return last

            def project_q(b, q, g):
                if isinstance(b, int):
                    pe.wait_ge(s_wl, q + 1)
                if q == 0:
                    pe.wait_ge(s_x, b + 1)
                wait(pe, s_qe, g)
                transposed(b, q, pQ, lambda c: c * 768).then_inc(s_q, 1)

            def project_k(b, q, g):
                wait(pe, s_ke, g)
                transposed(b, q, pK, lambda c: c * 768 + 256).then_inc(s_k, 1)

            def project_v(b, q, g):
                wait(pe, s_ve, g)
                for t in range(NT):
                    last = group(pV[:, t * T:(t + 1) * T],
                                 [(tokens(b, tk, c, t * P, P), weights(w, q, c * 768 + 512, QH * HD))
                                  for c in range(NC) for w, tk in PASSES])
                last.then_inc(s_v, 1)

            def project_gate(b, q, g):
                wait(pe, s_ge, g)
                transposed(b, q, pG, lambda c: QW + c * 256).then_inc(s_g, 1)

            def scores(q, h, u):
                if u == 0:
                    pe.wait_ge(s_q2, h + 1)
                    pe.wait_ge(s_k2, h + 1)
                    wait(pe, s_Sm, 2 * h)
                else:
                    pe.wait_ge(s_Sm, 2 * h + 1)
                i = q % 2
                for e in range(2):
                    group(pS0[:, e * T:(e + 1) * T],
                          [(k2[i][:, u, e, 0:P], a[i][:, u, e, :]) for a in (q2h, q2l)])
                    last = group(pS1[:, e * P:(e + 1) * P],
                                 [(k2[i][:, u, e, P:T], a[i][:, u, e, P:T]) for a in (q2h, q2l)])
                last.then_inc(s_S, 1)

            def attention(q, h):
                pe.wait_ge(s_Sm, 2 * h + 2)
                pe.wait_ge(s_ve, h + 1)
                wait(pe, s_sq, h)
                i = q % 2
                for u in range(2):
                    for t in range(NT):
                        for e in range(2):
                            head = 2 * u + e
                            last = nc.tensor.matmul(pC[64 * e:64 * e + 64, u * T + t * P:(u + 1) * T],
                                                    v32[i][:, t, head * HD:(head + 1) * HD],
                                                    S[:, head, 0:T] if t == 0 else S[:, head, T:T + P],
                                                    start=(t == 0), stop=(t == NT - 1))
                last.then_inc(s_C, 1)

            def output(b, q, h):
                pe.wait_ge(s_yl, h + 1)
                if q == 0:
                    wait(pe, s_oe, b)
                for u in range(2):
                    for t in range(NT):
                        for n, (w, y) in enumerate(PASSES):
                            last = nc.tensor.matmul(
                                pO[:, t * HID:(t + 1) * HID], (yh, yl)[y][:, u * T + t * P:u * T + (t + 1) * P],
                                Wo[:, w, q, u * HID:(u + 1) * HID], start=(q == 0 and u == 0 and t == 0 and n == 0),
                                stop=(q == NQ - 1 and u == 1 and n == 2), skip_group_check=True)
                last.then_inc(s_D, 1)

            def piece(b, q, h):
                if q in (1, 3, 4, 5, 6, 7):
                    wait(pe, s_sq, h)
                if q == 1:
                    pe.wait_ge(s_acc, 8 * b)
                    for t in range(NT):
                        last = group(pC[:, t:t + 1], [(acc[:, u * T + t * P:u * T + (t + 1) * P], ones[:, 0:1]) for u in range(2)])
                    last.then_inc(s_ss, 1)
                if q == 3:
                    pe.wait_ge(s_x1, b)
                    for t in range(NT):
                        for c in range(NC):
                            last = nc.tensor.transpose(pC[:, c * T + t * P:c * T + (t + 1) * P],
                                                       xr[:, t, c * P:(c + 1) * P], ident[:, :])
                    last.then_inc(s_T, 1)
                if q == 4:
                    pe.wait_ge(s_x1T, b)
                    for t in range(NT):
                        last = group(pC[:, t * EXP:(t + 1) * EXP],
                                     [(x1T[:, c, t * P:(t + 1) * P], wr[:, c, :]) for c in range(NC)])
                    last.then_inc(s_r, 1)
                if q == 5:
                    pe.wait_ge(s_th, b)
                    for s in range(2):
                        last = group(pC[0:FF, s * T:(s + 1) * T],
                                     [(wsh[:, c, s * FF:(s + 1) * FF], x1T[:, c, :]) for c in range(NC)])
                    last.then_inc(s_gu, 1)
                if q == 6:
                    pe.wait_ge(s_h, b)
                    pe.wait_ge(s_mask, b)
                    nc.tensor.matmul(pC[0:EXP, 0:T], mask[:, 0, :], triu[:, 0:T], start=True, stop=False)
                    nc.tensor.matmul(pC[0:EXP, P:T], mask[:, 1, :], triu[:, 0:P], start=False, stop=True).then_inc(s_cum, 1)
                if q == 7:
                    pe.wait_ge(s_cume, b)
                    for t in range(NT):
                        last = group(pC[:, t * HID:(t + 1) * HID], [(hT[:, t * P:(t + 1) * P], wsd[:, :])])
                    last.then_inc(s_dn, 1)

            def bank_of_attention(b, q):
                if q == 0:
                    wait(pe, s_bs, b)
                elif behind(b):
                    done = {2: s_sse, 4: s_x1T, 5: s_th, 6: s_h, 7: s_cume}.get(q)
                    if done is not None:
                        pe.wait_ge(done, b)

            def step(b, q):
                g = b * NQ + q
                if isinstance(b, int) and b == SEQS and q >= 2:
                    piece(b, q, STEPS)
                    return
                if has(g):
                    project_q(b, q, g)
                    project_k(b, q, g)
                if has(g - 2):
                    bank_of_attention(b, q)
                    attention((q - 2) % NQ, g - 2)
                if has(g):
                    project_v(b, q, g)
                    project_gate(b, q, g)
                if has(g - 1):
                    scores((q - 1) % NQ, g - 1, 0)
                if has(g - 2):
                    output(b, (q - 2) % NQ, g - 2)
                if has(g - 1):
                    scores((q - 1) % NQ, g - 1, 1)
                if behind(b):
                    piece(b, q, g - 1)

            pe.wait_ge(s_const, 16 * 8)
            pe.wait_ge(s_tri, 1)
            sequences(pe, step)

            pe.wait_ge(s_ids, 1)
            nc.tensor.matmul(pC[0:BANDS, 0:PAIRS], bands[:, :], pick[:, 2:2 + PAIRS], start=True, stop=True)
            nc.tensor.matmul(pO[0:CAP, 0:EXP], ids[:, :], ident[0:EXP, 0:EXP], start=True, stop=True).then_inc(s_idp, 1)

            def transpose_rows(p, r):
                pe.wait_ge(s_gath[r], 16 * (p // 4 + 1) if isinstance(p, int) else p * 4 + (16 - 4 * r))
                wait(pe, s_xgT, p - 1)
                for c in range(NC):
                    last = nc.tensor.transpose(pT[r % 2][:, c * P:c * P + BANDS], xg[:, r, c * P:(c + 1) * P],
                                               ident[0:BANDS, 0:BANDS])
                last.then_inc(s_mT, 1)

            def gate_up(p, r):
                pe.wait_ge(s_xgT, p + 1)
                pe.wait_ge(s_ring[r], 32 * (p // 4 + 1) if isinstance(p, int) else p * 8 + (32 - 8 * r))
                wait(pe, s_mh, p - 1)
                for s in range(2):
                    for e in range(2):
                        last = group(pH[r % 2][0:FF, (2 * s + e) * CAP:(2 * s + e + 1) * CAP],
                                     [(ring_gu[r][:, e, s, c, :], xgT[:, r % 2, c, 64 * e:64 * e + CAP]) for c in range(NC)])
                last.then_inc(s_mgu, 1)

            def down(p, r):
                pe.wait_ge(s_mh, p + 1)
                wait(pe, s_wo, p - 1)
                for e in range(2):
                    last = nc.tensor.matmul(pDn[r % 2][64 * e:64 * e + CAP, 0:HID], mh[:, r % 2, e * CAP:(e + 1) * CAP],
                                            ring_d[r][:, e, :], start=True, stop=True)
                last.then_inc(s_md, 1)

            def pairs(i):
                for r in range(RING):
                    p = RING * i + r
                    if not (isinstance(p, int) and p == PAIRS - 1):
                        transpose_rows(p + 1, (r + 1) % RING)
                    gate_up(p, r)
                    if not (isinstance(p, int) and p == 0):
                        down(p - 1, (r - 1) % RING)

            transpose_rows(0, 0)
            pairs(0)
            with pe.Fori(1, PAIRS // RING - 1) as i:
                pairs(i)
            pairs(PAIRS // RING - 1)
            down(PAIRS - 1, RING - 1)

        @block.scalar
        def _(act):
            def split_weights(Q):
                i = Q % 2
                act.wait_ge(s_stage[i], 32 * (Q // 2 + 1))
                nc.scalar.activation(Wv[:, 0, Q, :], stage[:, i, 0:QW + GW], ACT.Copy, scale=W_SCALE)
                for u in range(2):
                    a = QW + GW + u * HID
                    last = nc.scalar.activation(Wo[:, 0, Q, u * HID:(u + 1) * HID], stage[:, i, a:a + HID],
                                                ACT.Copy, scale=nw[:, 2 * Q + u:2 * Q + u + 1])
                last.then_inc(s_wh, 1)

            def act_q(q, g):
                act.wait_ge(s_q, g + 1)
                wait(act, s_q2, g)
                wait(act, s_S, 2 * (g - 1))
                nc.scalar.activation(q32[:, :, :], pQ[:, :].rearrange("p (u n) -> p u n", u=2), ACT.Silu, scale=1 / W_SCALE)
                for e, (a, z_) in enumerate(HALF):
                    src = pQ[a:z_, :].rearrange("p (u n) -> p u n", u=2)
                    for lo, hi in HALF:
                        last = nc.scalar.activation(q2h[q % 2][lo:hi, :, e, :], src, ACT.Silu, scale=1 / W_SCALE)
                last.then_inc(s_qe, 1)

            def act_k(q, g):
                act.wait_ge(s_k, g + 1)
                wait(act, s_k2, g)
                a, b_ = [pK[lo:hi, :].rearrange("p (u n) -> p u n", u=2) for lo, hi in HALF]
                nc.scalar.activation(k32[:, :, :], pK[:, :].rearrange("p (u n) -> p u n", u=2), ACT.Silu, scale=1 / W_SCALE)
                nc.scalar.activation(k2[q % 2][0:64, :, 0, :], a, ACT.Silu, scale=1 / W_SCALE)
                nc.scalar.activation(k2[q % 2][0:64, :, 1, :], b_, ACT.Silu, scale=1 / W_SCALE)
                nc.scalar.activation(khB[64:128, :, :], b_, ACT.Silu, scale=1 / W_SCALE).then_inc(s_ke, 1)

            def act_v(q, g):
                act.wait_ge(s_v, g + 1)
                wait(act, s_C, g - 1)
                nc.scalar.activation(v32[q % 2][:, :, :].rearrange("p t n -> p (t n)"), pV[:, :], ACT.Silu,
                                     scale=1 / W_SCALE).then_inc(s_ve, 1)

            def act_gate(q, g):
                act.wait_ge(s_g, g + 1)
                wait(act, s_y, g - 1)
                nc.scalar.activation(gt[q % 2][:, :], pG[:, :], ACT.Tanh, scale=0.5 / W_SCALE).then_inc(s_ge, 1)

            def act_y(h):
                act.wait_ge(s_y, h + 1)
                wait(act, s_D, h)
                nc.scalar.activation(yh[:, :], y32[:, :], ACT.Copy).then_inc(s_yh, 1)
                wait(act, s_acc, h)
                nc.scalar.activation(sq[:, :], pC[:, :], ACT.Square).then_inc(s_sq, 1)

            def piece(b, q):
                if q == 4:
                    act.wait_ge(s_T, b)
                    nc.scalar.activation(x1T[:, :, :].rearrange("p c n -> p (c n)"), pC[:, :], ACT.Copy).then_inc(s_x1T, 1)
                if q == 5:
                    act.wait_ge(s_r, b)
                    nc.scalar.activation(th[:, :, :].rearrange("p t n -> p (t n)"), pC[:, 0:NT * EXP], ACT.Tanh,
                                         scale=0.5).then_inc(s_th, 1)
                if q == 6:
                    act.wait_ge(s_gu, b)
                    nc.scalar.activation(hs[:, :], pC[0:FF, 0:T], ACT.Silu).then_inc(s_hs, 1)

            def step(b, q):
                g = b * NQ + q
                if behind(b):
                    piece(b, q)
                if isinstance(b, int) and b == 0 and q + 1 < NQ:
                    split_weights(q + 1)
                if has(g):
                    act_q(q, g)
                if has(g - 2):
                    act_y(g - 2)
                if has(g):
                    act_k(q, g)
                    act_v(q, g)
                    act_gate(q, g)

            act.wait_ge(s_nw, 1)
            split_weights(0)
            sequences(act, step)

            def evacuate(p, r):
                act.wait_ge(s_mT, p + 1)
                wait(act, s_mgu, p - 1)
                nc.scalar.activation(xgT[:, r % 2, :, :],
                                     pT[r % 2][:, 0:NC * P].rearrange("p (c n) -> p c n", c=NC)[:, :, 0:BANDS],
                                     ACT.Copy).then_inc(s_xgT, 1)

            def pairs(i):
                for r in range(RING):
                    p = RING * i + r
                    if not (isinstance(p, int) and p == PAIRS - 1):
                        evacuate(p + 1, (r + 1) % RING)
                    act.wait_ge(s_mgu, p + 1)
                    wait(act, s_mh, p - 1)
                    nc.scalar.activation(mhs[:, r % 2, :], pH[r % 2][0:FF, 0:2 * CAP], ACT.Silu).then_inc(s_mhs, 1)

            evacuate(0, 0)
            pairs(0)
            with act.Fori(1, PAIRS // RING - 1) as i:
                pairs(i)
            pairs(PAIRS // RING - 1)

            for c in range(TOK // P // FIN):
                act.wait_ge(s_nm, c + 1)
                for k in range(FIN):
                    last = nc.scalar.activation(f1[c % 4][:, k, :], f0[c % 4][:, k, :], ACT.Identity,
                                                scale=frs[:, c % 2, k:k + 1], bias=nmr[:, c % 2, k:k + 1])
                last.then_inc(s_fo, 1)

        @block.vector
        def _(dve):
            def split_weights(Q):
                i = Q % 2
                dve.wait_ge(s_wh, Q + 1)
                nc.vector.scalar_tensor_tensor(Wv[:, 1, Q, :], stage[:, i, 0:QW + GW], W_SCALE, Wv[:, 0, Q, :],
                                               ALU.mult, ALU.subtract)
                for u in range(2):
                    a = QW + GW + u * HID
                    cols = slice(u * HID, (u + 1) * HID)
                    last = nc.vector.scalar_tensor_tensor(Wo[:, 1, Q, cols], stage[:, i, a:a + HID],
                                                          nw[:, 2 * Q + u:2 * Q + u + 1], Wo[:, 0, Q, cols],
                                                          ALU.mult, ALU.subtract)
                last.then_inc(s_wl, 1)

            def gate(q, h):
                dve.wait_ge(s_C, h + 1)
                dve.wait_ge(s_ge, h + 1)
                nc.vector.scalar_tensor_tensor(y32[:, :], gt[q % 2][:, :], 1.0, pC[:, :], ALU.add, ALU.mult).then_inc(s_y, 1)

            def low_y(h):
                dve.wait_ge(s_yh, h + 1)
                nc.vector.tensor_tensor(yl[:, :], y32[:, :], yh[:, :], ALU.subtract).then_inc(s_yl, 1)

            def low_q(q, g):
                dve.wait_ge(s_qe, g + 1)
                h, l = q2h[q % 2], q2l[q % 2]
                nc.vector.tensor_tensor(l[0:64, :, 0, :], q32[0:64, :, :], h[0:64, :, 0, :], ALU.subtract)
                nc.vector.tensor_tensor(l[64:128, :, 1, :], q32[64:128, :, :], h[64:128, :, 1, :], ALU.subtract).then_inc(s_ql, 1)
                dve.wait_ge(s_ql, g + 1)
                nc.vector.tensor_copy(l[64:128, :, 0, :], l[0:64, :, 0, :])
                nc.vector.tensor_copy(l[0:64, :, 1, :], l[64:128, :, 1, :]).then_inc(s_q2, 1)

            def low_k(q, g):
                dve.wait_ge(s_ke, g + 1)
                k = k2[q % 2]
                nc.vector.tensor_tensor(k[64:128, :, 0, :], k32[0:64, :, :], k[0:64, :, 0, :], ALU.subtract)
                nc.vector.tensor_tensor(k[64:128, :, 1, :], k32[64:128, :, :], khB[64:128, :, :], ALU.subtract).then_inc(s_k2, 1)

            def decayed(b, q, h, u):
                dve.wait_ge(s_S, 2 * h + u + 1)
                if isinstance(b, int) and u == 0 and b == 0:
                    dve.wait_ge(s_stage[q % 2], 32 * (q // 2 + 1))
                d = D[:, q, :].rearrange("p (h n) -> p h n", h=QH)[:, 2 * u:2 * u + 2, :]
                nc.vector.tensor_tensor(S[:, 2 * u:2 * u + 2, 0:T], pS0[:, :].rearrange("p (h n) -> p h n", h=2), d, ALU.mult)
                nc.vector.tensor_tensor(S[:, 2 * u:2 * u + 2, T:T + P], pS1[:, 0:2 * P].rearrange("p (h n) -> p h n", h=2),
                                        d[:, :, 0:P], ALU.mult).then_inc(s_Sm, 1)

            def norm_sums(b):
                f = (2 * W_SCALE) ** 2
                dve.wait_ge(s_ss, b)
                nc.vector.tensor_scalar(ssv[:, :], pC[:, 0:NT], f / INNER, f * EPS, ALU.mult, ALU.add).then_inc(s_sse, 1)

            def residual(b):
                chain = Chain(dve, s_ln1, LN1_LINKS * (b - 1), s_dve_passed)
                dve.wait_ge(s_rstd1, b)
                dve.wait_ge(s_xn, 16 * b)
                for t in range(NT):
                    last = nc.vector.scalar_tensor_tensor(z[:, t, :], o32[:, t, :], rstd1[:, t:t + 1], xn[:, t, :], ALU.mult, ALU.add)
                last.then_inc(s_z, 1)
                dve.wait_ge(s_z, b + 1)
                for t in range(NT):
                    last = nc.vector.bn_stats(st6[:, t, :], z[:, t, :])
                chain.link(last)
                for t in range(NT):
                    last = nc.vector.bn_aggr(mv[:, t, :], st6[:, t, :])
                chain.link(last)
                last = nc.vector.tensor_scalar(vv[:, 0:NT], mv[:, 0:NT, 1], EPS, None, ALU.add)
                chain.link(last)
                nc.vector.tensor_copy(ssv[:, :], vv[:, 0:NT]).then_inc(s_var, 1)
                assert chain.n == LN1_LINKS

            def normed(b):
                dve.wait_ge(s_rstd2, b)
                dve.wait_ge(s_rows, 16 * b)
                for t in range(NT):
                    last = nc.vector.tensor_scalar(xr[:, t, 0:HID], z[:, t, :], mv[:, t, 0:1], rstd2[:, t:t + 1],
                                                   ALU.subtract, ALU.mult)
                last.then_inc(s_x1, 1)

            route = {}

            def route_groups(b):
                chain = route["chain"] = Chain(dve, s_route, ROUTE_LINKS * (b - 1), s_dve_passed)
                dve.wait_ge(s_th, b)
                chain.link(nc.vector.tensor_scalar(sc[:, :, :], th[:, :, :], 0.5, 0.5, ALU.mult, ALU.add))
                chain.link(nc.vector.tensor_tensor(scb[:, :, :], sc[:, :, :], b2[:, :, :], ALU.add))
                by_group = scb[:, :, :].rearrange("p t (g e) -> p (t g) e", g=GROUPS)
                for k in range(NT * GROUPS):
                    last = nc.vector.max(top[:, k, :], by_group[:, k, :])
                chain.link(last)
                best = top[:, :, :].rearrange("p (t g) e -> p t g e", t=NT)
                chain.link(nc.vector.tensor_tensor(gs[:, :, 0:GROUPS], best[:, :, :, 0], best[:, :, :, 1], ALU.add))
                for t in range(NT):
                    last = nc.vector.max(g8[:, t, :], gs[:, t, :])
                chain.link(last)
                chain.link(nc.vector.memset(g8[:, :, TOPG:8], NEG))
                for t in range(NT):
                    last = nc.vector.match_replace(grep[:, t, :], g8[:, t, :], gs[:, t, :], NEG)
                chain.link(last)
                chain.link(nc.vector.tensor_tensor(uns[:, :, :], grep[:, :, 0:GROUPS], gs[:, :, 0:GROUPS], ALU.is_equal))

            def route_experts(b):
                chain = route["chain"]
                out3 = [a[:, :, :].rearrange("p t (g e) -> p (t g) e", g=GROUPS) for a in (masked, scb)]
                dropped = uns[:, :, :].rearrange("p t g -> p (t g)").unsqueeze(2).broadcast_to([P, NT * GROUPS, EXP // GROUPS])
                chain.link(nc.vector.scalar_tensor_tensor(out3[0], dropped, NEG, out3[1], ALU.mult, ALU.add))
                for t in range(NT):
                    last = nc.vector.max(t8[:, t, :], masked[:, t, :])
                chain.link(last)
                chain.link(nc.vector.memset(t8[:, :, TOPK:8], NEG))
                for t in range(NT):
                    last = nc.vector.match_replace(mrep[:, t, :], t8[:, t, :], masked[:, t, :], NEG)
                chain.link(last)
                nc.vector.tensor_tensor(mask[:, :, :], mrep[:, :, :], masked[:, :, :], ALU.not_equal).then_inc(s_mask, 1)
                dve.wait_ge(s_mask, b)
                for t in range(NT):
                    last = nc.vector.scalar_tensor_tensor(wsel[:, t, :], mask[:, t, :], 1.0, sc[:, t, :], ALU.mult, ALU.mult,
                                                          accum_out=wsum[:, t:t + 1])
                chain.link(last)
                chain.link(nc.vector.reciprocal(wrec[:, :], wsum[:, :]))
                for t in range(NT):
                    last = nc.vector.tensor_scalar(xr[:, t, HID:ROW], wsel[:, t, :], wrec[:, t:t + 1], ROUTE_SCALE,
                                                   ALU.mult, ALU.mult)
                last.then_inc(s_w, 1)
                assert chain.n == ROUTE_LINKS, chain.n

            def running_counts(b):
                dve.wait_ge(s_cum, b)
                nc.vector.tensor_scalar(cumb[:, 0:T], pC[0:EXP, 0:T], carry[:, 0:1], None, ALU.add).then_inc(s_cume, 1)

            def find_slots(b):
                chain = Chain(dve, s_find, FIND_LINKS * (b - 1), s_dve_passed)
                wait_apart(dve, s_dve_passed, (s_cume, b))
                for k in range(0, CAP, 8):
                    nc.vector.max_index(found[:, k:k + 8], vals[:, k:k + 8], cumb[:, :])
                chain.link(nc.vector.tensor_copy(carry[:, :], cumb[:, T - 1:T]))
                chain.link(nc.vector.tensor_copy(foundf[:, :], found[:, :]))
                chain.link(nc.vector.tensor_scalar(pen[:, :], foundf[:, :], float(T), FAR, ALU.is_ge, ALU.mult))
                chain.link(nc.vector.scalar_tensor_tensor(cand[:, :], foundf[:, :], first[:, 0:1], pen[:, :], ALU.add, ALU.add))
                nc.vector.tensor_tensor(ids[:, :], ids[:, :], cand[:, :], ALU.min)
                chain.link(nc.vector.tensor_scalar(first[:, :], first[:, :], float(T), None, ALU.add))
                assert chain.n == FIND_LINKS, chain.n

            def step(b, q):
                g = b * NQ + q
                if behind(b):
                    if q == 2:
                        norm_sums(b)
                    if q == 3:
                        normed(b)
                    if q == 6:
                        dve.wait_ge(s_hs, b)
                        nc.vector.tensor_tensor(hT[:, :], hs[:, :], pC[0:FF, T:2 * T], ALU.mult).then_inc(s_h, 1)
                    if q == 7:
                        running_counts(b)
                if isinstance(b, int) and b == 0 and q + 1 < NQ:
                    split_weights(q + 1)
                if has(g - 2):
                    gate((q - 2) % NQ, g - 2)
                if has(g):
                    low_q(q, g)
                if has(g - 2):
                    low_y(g - 2)
                if has(g - 1):
                    decayed(b, (q - 1) % NQ, g - 1, 0)
                if has(g):
                    low_k(q, g)
                if behind(b):
                    if q == 2:
                        residual(b)
                    if q == 5:
                        route_groups(b)
                    if q == 6:
                        route_experts(b)
                    if q == 7:
                        find_slots(b)
                if behind(b) and q == 1:
                    dve.wait_ge(s_D, 8 * b)
                    nc.vector.tensor_copy(o32[:, :, :].rearrange("p t n -> p (t n)"), pO[:, :]).then_inc(s_oe, 1)
                if has(g - 1):
                    decayed(b, (q - 1) % NQ, g - 1, 1)
                if behind(b) and q == 7:
                    dve.wait_ge(s_dn, b)
                    dve.wait_ge(s_base, 16 * b)
                    nc.vector.tensor_tensor(bs[:, :, :], pC[:, :].rearrange("p (t n) -> p t n", t=NT), xr[:, :, 0:HID],
                                            ALU.add).then_inc(s_bs, 1)

            nc.vector.memset(zeros[:, :], 0.0).then_inc(s_init, 1)
            nc.vector.memset(z[:, :, :], 0.0).then_inc(s_z, 1)
            nc.vector.memset(bs[:, :, :], 0.0).then_inc(s_bs, 1)
            for a, value in ((ones[:, :], 1.0), (gs[:, :, :], NEG), (carry[:, :], 0.0), (first[:, :], 0.0),
                             (bands[:, :], 0.0), (ids[:, :], 4 * FAR)):
                nc.vector.memset(a, value)
            dve.wait_ge(s_const, 16 * 8)
            nc.vector.tensor_scalar(nw[:, :], nw[:, :], W_SCALE, None, ALU.mult).then_inc(s_nw, 1)
            nc.vector.tensor_copy(triu[:, :], triu32[:, :]).then_inc(s_tri, 1)
            dve.wait_ge(s_mhalf, 3)
            nc.vector.tensor_copy(cumb[:, T:T + CAP], vals[:, :])
            split_weights(0)
            sequences(dve, step)

            chain = Chain(dve, s_slots, 0)
            chain.link(nc.vector.tensor_tensor(ids[:, :], ids[:, :], dummy[:, :], ALU.min))
            chain.link(nc.vector.tensor_scalar(idsg[:, :], ids[:, :], float(TOK - 1), None, ALU.min))
            for e in range(2):
                last = nc.vector.tensor_scalar(bands[:, 64 * e:64 * e + CAP], idsg[:, :], pick[:, e:e + 1], None, ALU.mult)
            last.then_inc(s_ids, 1)
            dve.wait_ge(s_idp, 1)
            nc.vector.tensor_copy(gidx[:, :], pC[0:BANDS, 0:PAIRS])
            nc.vector.tensor_copy(sidx[:, :], pO[0:CAP, 0:EXP]).then_inc(s_idx, 1)
            dve.wait_ge(s_idx, 1)

            def gather_column(p, r):
                nc.vector.tensor_copy(gcol[:, r:r + 1], gidx[:, bass.ds(p, 1)]).then_inc(s_gcol, 1)

            def weigh(p, r):
                dve.wait_ge(s_md, p + 1)
                for e in range(2):
                    wait(dve, s_sc[e], 16 * (p - 1))
                for e in range(2):
                    a = 64 * e
                    last = nc.vector.tensor_scalar(wo[:, r % 2, e, :], pDn[r % 2][a:a + CAP, 0:HID],
                                                   xg[a:a + CAP, r, bass.ds(2 * p + (HID + e), 1)], None, ALU.mult)
                last.then_inc(s_wo, 1)

            def pairs(i):
                for r in range(RING):
                    p = RING * i + r
                    dve.wait_ge(s_mhs, p + 1)
                    wait(dve, s_md, p - 1)
                    nc.vector.tensor_tensor(mh[:, r % 2, :], mhs[:, r % 2, :], pH[r % 2][0:FF, 2 * CAP:4 * CAP],
                                            ALU.mult).then_inc(s_mh, 1)
                    nc.vector.tensor_copy(scol[:, r, :], sidx[:, bass.ds(2 * p, 2)])
                    if not (isinstance(p, int) and p == 0):
                        weigh(p - 1, (r - 1) % RING)
                    if not (isinstance(p, int) and p + 3 >= PAIRS):
                        gather_column(p + 3, (r + 3) % 4)

            for p in range(3):
                gather_column(p, p)
            pairs(0)
            with dve.Fori(1, PAIRS // RING - 1) as i:
                pairs(i)
            pairs(PAIRS // RING - 1)
            weigh(PAIRS - 1, RING - 1)

            chunks = TOK // P // FIN
            chain = Chain(dve, s_fin, 0)
            for c in range(chunks + 1):
                if c < chunks:
                    dve.wait_ge(s_fl[c % 4], 32 * (c // 4 + 1))
                    if c >= 2:
                        dve.wait_ge(s_fo, c - 1)
                    chain.link(nc.vector.tensor_tensor(f0[c % 4], f0[c % 4], f1[c % 4], ALU.add))
                    for k in range(FIN):
                        last = nc.vector.bn_stats(st6[:, k, :], f0[c % 4][:, k, :])
                    chain.link(last)
                    for k in range(FIN):
                        last = nc.vector.bn_aggr(fmv[:, c % 2, k, :], st6[:, k, :])
                    chain.link(last)
                if c >= 1:
                    dve.wait_ge(s_frs, c)
                    nc.vector.scalar_tensor_tensor(nmr[:, (c - 1) % 2, :], fmv[:, (c - 1) % 2, :, 0], -1.0, frs[:, (c - 1) % 2, :],
                                                   ALU.mult, ALU.mult).then_inc(s_nm, 1)
                if c < chunks:
                    nc.vector.tensor_scalar(vv[:, :], fmv[:, c % 2, :, 1], EPS, None, ALU.add).then_inc(s_fv, 1)

        @block.gpsimd
        def _(pool):
            def split_tokens(b):
                at = (b % 2) * (NC * T)
                waits = [(s_xin, 16 * (b + 1))]
                if not (isinstance(b, int) and b < 2):
                    waits.append((s_g, NQ * (b - 1)))
                wait_apart(pool, s_pool_passed, *waits)
                nc.gpsimd.tensor_copy(xh[:, bass.ds(at, NC * T)], xs[:, :]).then_inc(s_xh, 1)
                pool.wait_ge(s_xh, b + 1)
                nc.gpsimd.tensor_tensor(xl[:, bass.ds(at, NC * T)], xs[:, :], xh[:, bass.ds(at, NC * T)], ALU.subtract).then_inc(s_x, 1)

            def add_squares(b, q, h):
                if q == 0:
                    wait_apart(pool, s_pool_passed, (s_sq, h + 1), (s_ss, b))
                    nc.gpsimd.tensor_copy(acc[:, :], sq[:, :]).then_inc(s_acc, 1)
                else:
                    pool.wait_ge(s_sq, h + 1)
                    pool.wait_ge(s_acc, h)
                    nc.gpsimd.tensor_tensor(acc[:, :], acc[:, :], sq[:, :], ALU.add).then_inc(s_acc, 1)

            def step(b, q):
                g = b * NQ + q
                last_b = isinstance(b, int) and b == SEQS
                if behind(b) and q == 2:
                    pool.wait_ge(s_sse, b)
                    nc.gpsimd.tensor_tensor(rstd1[:, :], ssv[:, :], mhalf[:, 0:NT], ALU.pow).then_inc(s_rstd1, 1)
                if has(g - 2):
                    add_squares(b, (q - 2) % NQ, g - 2)
                if behind(b) and q == 2:
                    pool.wait_ge(s_var, b)
                    nc.gpsimd.tensor_tensor(rstd2[:, 0:NT], vv[:, 0:NT], mhalf[:, 0:NT], ALU.pow).then_inc(s_rstd2, 1)
                if q == 3 and not last_b:
                    split_tokens(b + 1)

            nc.gpsimd.memset(mhalf[:, :], -0.5).then_inc(s_mhalf, 1)
            nc.gpsimd.iota(vals[:, :], [[1, CAP]], base=1, channel_multiplier=0, allow_small_or_imprecise_dtypes=True).then_inc(s_mhalf, 1)
            nc.gpsimd.iota(dummy[:, :], [[1, CAP]], base=TOK, channel_multiplier=0, allow_small_or_imprecise_dtypes=True).then_inc(s_mhalf, 1)
            split_tokens(0)
            sequences(pool, step)

            def gather(p, r):
                wait_apart(pool, s_pool_passed, (s_gcol, p + 1), (s_wo, p - 3))
                nc.gpsimd.indirect_dma_start(xg[:, r, :], None, grows[:, :],
                                             bass.IndirectOffsetOnAxis(ap=gcol[:, r:r + 1], axis=0)).then_inc(s_gath[r], 16)

            def pairs(i):
                for r in range(RING):
                    p = RING * i + r
                    if not (isinstance(p, int) and p + 3 >= PAIRS):
                        gather(p + 3, (r + 3) % 4)
                    for e in range(2):
                        wait_apart(pool, s_pool_passed, (s_wo, p + 1), (s_sc[e], 16 * p))
                        nc.gpsimd.indirect_dma_start(sums[e][:, :], bass.IndirectOffsetOnAxis(ap=scol[:, r, e:e + 1], axis=0),
                                                     wo[:, r % 2, e, :], None, compute_op=ALU.add).then_inc(s_sc[e], 16)

            pool.wait_ge(s_rows, 16 * (SEQS + 1))
            for p in range(3):
                gather(p, p)
            pool.wait_ge(s_base, 16 * (SEQS + 1))
            pool.wait_ge(s_zero, 16)
            pairs(0)
            with pool.Fori(1, PAIRS // RING - 1) as i:
                pairs(i)
            pairs(PAIRS // RING - 1)

            for c in range(TOK // P // FIN):
                pool.wait_ge(s_fv, c + 1)
                nc.gpsimd.tensor_tensor(frs[:, c % 2, :], vv[:, :], mhalf[:, :], ALU.pow).then_inc(s_frs, 1)


def kernel(**inputs):
    import numpy as np
    import concourse.bacc as bacc
    from concourse.bass_utils import run_bass_kernel_spmd

    a = {k: np.asarray(v) for k, v in inputs.items()}
    x = np.ascontiguousarray(a["L0_attn_hidden_states"]).reshape(TOK, HID)
    qkv = a["L0_attn_qkv_w"].reshape(NQ, QH, 3, HD, NC, P).transpose(0, 5, 4, 2, 1, 3).reshape(NQ, P, QW)
    gate = a["L0_attn_gate_w"].reshape(NQ, QH * HD, NC, P).transpose(0, 3, 2, 1).reshape(NQ, P, GW)
    wout = a["L0_attn_out_w"].reshape(HID, NQ, 2, P).transpose(1, 3, 2, 0).reshape(NQ, P, OW)
    slope = ((1.0 / 2.0 ** (8.0 / HEADS)) ** (np.arange(HEADS, dtype=np.float32) + np.float32(1.0))).astype(np.float32)
    slope = (slope * np.float32(1.0 - 0 / (32 - 1 + 1e-05) + 1e-05)).astype(np.float32)
    dist = np.arange(T)[None, :] - np.arange(P)[:, None]
    decay = np.where(dist >= 0, np.exp(-slope.astype(np.float64)[:, None, None] * np.maximum(dist, 0)), 0.0).astype(np.float32)
    decay = decay.reshape(NQ, QH, P, T).transpose(0, 2, 1, 3).reshape(NQ, P, QH * T)
    tri = np.concatenate([np.triu(np.ones((P, P), np.float32)), np.ones((P, T - P), np.float32)], axis=1)
    e = np.arange(EXP)
    pair_pick = np.concatenate([(e[:, None] % 2 == np.arange(2)[None, :]),
                                (e[:, None] // 2 == np.arange(PAIRS)[None, :])], axis=1).astype(np.float32)
    by_chunk = lambda w: w.reshape(NC, P, -1).transpose(1, 0, 2)
    gu = np.stack([a["L0_ffn_w_gate"], a["L0_ffn_w_up"]], axis=1).reshape(PAIRS, 2, 2, NC, P, FF)
    arrays = {
        "x": x,
        "xT": x.T,
        "wprep": np.concatenate([qkv, gate, wout], axis=2),
        "normw": a["L0_attn_norm_w"].reshape(HEADS // 2, P).T,
        "decay": decay,
        "eye": np.eye(P, dtype=np.float32),
        "tri": tri,
        "w_router": by_chunk(a["L0_ffn_gate_w"]),
        "bias2": np.broadcast_to(a["L0_ffn_bias"][None, None, :], (P, NT, EXP)),
        "w_shared": by_chunk(np.concatenate([a["L0_ffn_ws_gate"], a["L0_ffn_ws_up"]], axis=1)),
        "w_shared_down": a["L0_ffn_ws_down"],
        "w_experts": gu.transpose(0, 4, 1, 2, 3, 5).reshape(PAIRS, P, 4 * NC * FF),
        "w_down": a["L0_ffn_w_down"].reshape(PAIRS, 2, FF, HID).transpose(0, 2, 1, 3).reshape(PAIRS, FF, 2 * HID),
        "pair_pick": pair_pick,
    }
    arrays = {k: np.ascontiguousarray(v) for k, v in arrays.items()}
    nc = bacc.Bacc("TRN2", target_bir_lowering=False, num_devices=1)
    aps = {k: nc.dram_tensor(k, v.shape, mybir.dt.from_np(v.dtype), kind="ExternalInput").ap() for k, v in arrays.items()}
    out = nc.dram_tensor("out", (TOK, HID), F32, kind="ExternalOutput").ap()
    block_kernel(nc, **aps, out=out)
    r = run_bass_kernel_spmd(nc, [arrays], core_ids=[0])
    return r.results[0]["out"].reshape(SEQS, T, HID)
```

```python
import concourse.bass as bass
from concourse import mybir
from contextlib import ExitStack

F32 = mybir.dt.float32
F16 = mybir.dt.float16
U32 = mybir.dt.uint32
ALU = mybir.AluOpType
ACT = mybir.ActivationFunctionType

P = 128
SEQS, T, HID = 16, 256, 256
TOK = SEQS * T
HEADS, HD = 32, 64
INNER = HEADS * HD
QH = 4
NQ = HEADS // QH
STEPS = SEQS * NQ
NT = T // P
NC = HID // P
QW, GW, OW = NC * 3 * 256, NC * 256, 2 * HID
PREP = QW + GW + OW
W_SCALE = 1024.0
EPS = 1e-5
EXP, TOPK, GROUPS, TOPG, FF = 64, 6, 8, 4, 96
CAP = 2 * ((2 * 128) * TOPK // EXP)
ROUTE_SCALE = 2.5
PAIRS = EXP // 2
ROW = HID + EXP
BANDS = 112
BAND = 64
NEG = -1e30
FAR = 8192.0
RING = 4
PAIR_W = 2 * 2 * NC * FF + 2 * HID
FIN = 4
FINALS = TOK // P // FIN
LN1_LINKS, ROUTE_LINKS, FIND_LINKS = 3, 14, 5


PARTS = 4
PART = NC * 256
EARLY = 2


def parts_split(quad, part):
    steps = PARTS + 1 if quad < EARLY else 2
    before = quad * (PARTS + 1) if quad < EARLY else EARLY * (PARTS + 1) + (quad - EARLY) * 2
    return before + (part + 1 if quad < EARLY else (1 if part < PARTS else steps))


def split_ranges(quad):
    return [(i * PART, (i + 1) * PART) for i in range(PARTS)] if quad < EARLY else [(0, PARTS * PART)]


def wait(eng, sem, value):
    if not (isinstance(value, int) and value <= 0):
        eng.wait_ge(sem, value)


def wait_apart(eng, passed, *waits):
    for sem, v in waits:
        wait(eng, sem, v)
    eng.sem_inc(passed, 1)


class Chain:

    def __init__(self, eng, sem, before, passed=None):
        self.eng, self.sem, self.before, self.n, self.passed = eng, sem, before, 0, passed

    def link(self, instruction):
        self.n += 1
        instruction.then_inc(self.sem, 1)
        if self.passed is None:
            self.eng.wait_ge(self.sem, self.before + self.n)
        else:
            wait_apart(self.eng, self.passed, (self.sem, self.before + self.n))


def block_kernel(nc, x, xT, wprep, normw, decay, eye, tri, w_router, bias2, w_shared, w_shared_down,
                 w_experts, w_down, slot_consts, out):
    grows = nc.dram_tensor("gather_rows", (TOK, ROW), F32, kind="Internal").ap()
    sums = nc.dram_tensor("sums", (2 * TOK + P, HID), F32, kind="Internal").ap()
    x_t = x.rearrange("(b t p) n -> b p t n", t=NT, p=P)
    xT_t = xT.rearrange("(c p) (b n) -> b p c n", p=P, b=SEQS)
    rows_t = grows.rearrange("(b t p) n -> b p t n", t=NT, p=P)
    base_t = sums[0:TOK, :].rearrange("(b t p) n -> b p t n", t=NT, p=P)

    with ExitStack() as ctx:
        def sb(name, shape, dt=F32):
            return ctx.enter_context(nc.sbuf_tensor(f"sb_{name}", shape, dt))

        def sem(name):
            return ctx.enter_context(nc.semaphore(name))

        W = sb("W", [P, 2 * NQ * (QW + GW)], F16)
        Wv = W[:, :].rearrange("p (s q n) -> p s q n", s=2, q=NQ)
        Wo = sb("Wo", [P, 2, NQ, OW], F16)
        stage = sb("stage", [P, 2, PREP])
        D = sb("D", [P, NQ, QH * T])
        nw = sb("nw", [P, HEADS // 2])
        xs = sb("xs", [P, NC * T])
        xh = sb("xh", [P, 2 * NC * T], F16)
        xl = sb("xl", [P, 2 * NC * T], F16)
        xn = sb("xn", [P, NT, HID])
        q32 = sb("q32", [P, 2, T])
        k32 = sb("k32", [P, 2, T])
        q2h = [sb(f"q2h{i}", [P, 2, 2, T], F16) for i in range(2)]
        q2l = [sb(f"q2l{i}", [P, 2, 2, T], F16) for i in range(2)]
        k2 = [sb(f"k2{i}", [P, 2, 2, T], F16) for i in range(2)]
        khB = sb("khB", [P, 2, T], F16)
        v32 = [sb(f"v32{i}", [P, NT, QH * HD]) for i in range(2)]
        gt = [sb(f"gt{i}", [P, 2 * T]) for i in range(2)]
        S = sb("S", [P, QH, T + P])
        y32 = sb("y32", [P, 2 * T])
        yh = sb("yh", [P, 2 * T], F16)
        yl = sb("yl", [P, 2 * T], F16)
        sq = sb("sq", [P, 2 * T])
        acc = sb("acc", [P, 2 * T])
        o32 = sb("o32", [P, NT, HID])
        z = sb("z", [P, NT, HID])
        ssv = sb("ssv", [P, NT])
        rstd1 = sb("rstd1", [P, NT])
        mhalf = sb("mhalf", [P, FIN])
        st6 = sb("st6", [P, 2, FIN, 6])
        mv = sb("mv", [P, FIN, 2])
        vv = sb("vv", [P, FIN])
        rstd2 = sb("rstd2", [P, FIN])
        nmr = sb("nmr", [P, 2, FIN])
        frs = sb("frs", [P, 2, FIN])
        fmv = sb("fmv", [P, 2, FIN, 2])
        xr = sb("xr", [P, NT, ROW])
        x1T = sb("x1T", [P, NC, T])
        wr = sb("wr", [P, NC, EXP])
        wsh = sb("wsh", [P, NC, 2 * FF])
        wsd = sb("wsd", [FF, HID])
        b2 = sb("b2", [P, NT, EXP])
        ident = sb("ident", [P, P])
        triu = sb("triu", [P, T], F16)
        triu32 = sb("triu32", [P, T])
        ones = sb("ones", [P, 1])
        th = sb("th", [P, NT, EXP])
        sc = sb("sc", [P, NT, EXP])
        scb = sb("scb", [P, NT, EXP])
        top = sb("top", [P, NT * GROUPS, 8])
        gs = sb("gs", [P, NT, 2 * GROUPS])
        g8 = sb("g8", [P, NT, 8])
        grep = sb("grep", [P, NT, 2 * GROUPS])
        uns = sb("uns", [P, NT, GROUPS])
        masked = sb("masked", [P, NT, EXP])
        t8 = sb("t8", [P, NT, 8])
        mrep = sb("mrep", [P, NT, EXP])
        mask = sb("mask", [P, NT, EXP], F16)
        wsel = sb("wsel", [P, NT, EXP])
        wsum = sb("wsum", [P, NT])
        wrec = sb("wrec", [P, NT])
        hs = sb("hs", [FF, T])
        hT = sb("hT", [FF, T])
        bs = sb("bs", [P, NT, HID])
        cumb = sb("cumb", [EXP, T + CAP])
        carry = sb("carry", [EXP, 1])
        vals = sb("vals", [EXP, CAP])
        found = sb("found", [EXP, CAP], U32)
        foundf = sb("foundf", [EXP, CAP])
        pen = sb("pen", [EXP, CAP])
        cand = sb("cand", [EXP, CAP])
        ids = sb("ids", [EXP, BAND])
        idsg = sb("idsg", [EXP, BAND])
        idss = sb("idss", [EXP, BAND])
        first = sb("first", [EXP, 1])
        slotc = sb("slotc", [EXP, 3 + PAIRS + BAND])
        pick, pairof, region, dummy = (slotc[:, 0:2], slotc[:, 2:2 + PAIRS], slotc[:, 2 + PAIRS:3 + PAIRS],
                                       slotc[:, 3 + PAIRS:3 + PAIRS + BAND])
        bandg = sb("bandg", [EXP, BANDS])
        bands = sb("bands", [EXP, BANDS])
        gidx = sb("gidx", [BANDS, PAIRS], U32)
        sidx = sb("sidx", [BANDS, PAIRS], U32)
        gcol = sb("gcol", [BANDS, 4], U32)
        scol = sb("scol", [BANDS, 4], U32)
        zeros = sb("zeros", [P, HID])
        flat = stage[:, :, :].rearrange("p s n -> p (s n)")
        xg = flat[0:BANDS, 0:4 * ROW].rearrange("p (s n) -> p s n", s=4)
        wo = flat[0:BANDS, 1280:1792].rearrange("p (s n) -> p s n", s=2)
        xgT = flat[:, 2304:2752].rearrange("p (s c n) -> p s c n", s=2, c=NC)
        mhs = flat[0:FF, 2752:2944].rearrange("p (s n) -> p s n", s=2)
        mh = flat[0:FF, 2944:3136].rearrange("p (s n) -> p s n", s=2)
        W32 = W[:, :].bitcast(F32)
        ring = [W32[:, r * PAIR_W:(r + 1) * PAIR_W] for r in range(RING)]
        ring_gu = [s[:, 0:4 * NC * FF].rearrange("p (e g c f) -> p e g c f", e=2, g=2, c=NC) for s in ring]
        ring_d = [s[0:FF, 4 * NC * FF:PAIR_W].rearrange("p (e n) -> p e n", e=2) for s in ring]
        D1 = D[:, :, :].rearrange("p q n -> p (q n)")
        CHUNK = FIN * HID
        f0 = [D1[:, c * CHUNK:(c + 1) * CHUNK].rearrange("p (k n) -> p k n", k=FIN) for c in range(FINALS)]
        behind_ring = W32[:, RING * PAIR_W:RING * PAIR_W + FINALS * CHUNK]
        f1 = [behind_ring[:, c * CHUNK:(c + 1) * CHUNK].rearrange("p (k n) -> p k n", k=FIN) for c in range(FINALS)]

        pQ, pK, pV, pG, pS0, pS1, pC, pO = [
            ctx.enter_context(nc.psum_tensor(n, [P, 512], F32))
            for n in ("pQ", "pK", "pV", "pG", "pS0", "pS1", "pC", "pO")]
        pT, pH, pDn = [pQ, pG], [pK, pS0], [pV, pS1]

        s_dve_passed, s_pool_passed = sem("s_dve_passed"), sem("s_pool_passed")
        s_const = sem("s_const")
        s_init = sem("s_init")
        s_tri = sem("s_tri")
        s_nwin, s_nw = sem("s_nwin"), sem("s_nw")
        s_mhalf = sem("s_mhalf")
        s_part = [sem(f"s_part{i}") for i in range(PARTS)]
        s_stage = [sem(f"s_stage{i}") for i in range(2)]
        s_decay = [sem(f"s_decay{i}") for i in range(2)]
        s_wh, s_wl = sem("s_wh"), sem("s_wl")
        s_xin = sem("s_xin")
        s_xh = sem("s_xh")
        s_x = sem("s_x")
        s_xn = sem("s_xn")
        s_q, s_k, s_v, s_g = sem("s_q"), sem("s_k"), sem("s_v"), sem("s_g")
        s_qe, s_ke, s_ve, s_ge = sem("s_qe"), sem("s_ke"), sem("s_ve"), sem("s_ge")
        s_ql = sem("s_ql")
        s_q2 = sem("s_q2")
        s_k2 = sem("s_k2")
        s_S = sem("s_S")
        s_Sm = sem("s_Sm")
        s_C = sem("s_C")
        s_y = sem("s_y")
        s_yh, s_yl = sem("s_yh"), sem("s_yl")
        s_sq = sem("s_sq")
        s_acc = sem("s_acc")
        s_D = sem("s_D")
        s_oe = sem("s_oe")
        s_ss, s_sse = sem("s_ss"), sem("s_sse")
        s_rstd1 = sem("s_rstd1")
        s_ln1 = sem("s_ln1")
        s_z = sem("s_z")
        s_var, s_rstd2 = sem("s_var"), sem("s_rstd2")
        s_x1 = sem("s_x1")
        s_T, s_x1T = sem("s_T"), sem("s_x1T")
        s_r, s_th = sem("s_r"), sem("s_th")
        s_route = sem("s_route")
        s_mask, s_w = sem("s_mask"), sem("s_w")
        s_gu, s_hs, s_h = sem("s_gu"), sem("s_hs"), sem("s_h")
        s_dn, s_bs = sem("s_dn"), sem("s_bs")
        s_cum, s_cume = sem("s_cum"), sem("s_cume")
        s_find = sem("s_find")
        s_rows, s_base = sem("s_rows"), sem("s_base")
        s_zero = sem("s_zero")
        s_ids, s_idp, s_idx = sem("s_ids"), sem("s_idp"), sem("s_idx")
        s_slots = sem("s_slots")
        s_gcol = sem("s_gcol")
        s_ring = [sem(f"s_ring{i}") for i in range(RING)]
        s_gath = [sem(f"s_gath{i}") for i in range(4)]
        s_mT, s_xgT = sem("s_mT"), sem("s_xgT")
        s_mgu, s_mhs, s_mh = sem("s_mgu"), sem("s_mhs"), sem("s_mh")
        s_md, s_wo = sem("s_md"), sem("s_wo")
        s_sc = sem("s_sc")
        s_fl = [sem(f"s_fl{i}") for i in range(FINALS)]
        s_fadd, s_fst, s_fag = sem("s_fadd"), sem("s_fst"), sem("s_fag")
        s_fv, s_frs, s_nm, s_fo, s_out = sem("s_fv"), sem("s_frs"), sem("s_nm"), sem("s_fo"), sem("s_out")

        block = ctx.enter_context(nc.Block())
        HALF = [(0, 64), (64, 128)]

        def has(g):
            return not isinstance(g, int) or 0 <= g < STEPS

        def sequences(eng, step):
            for q in range(NQ):
                step(0, q)
            with eng.Fori(1, SEQS) as b:
                for q in range(NQ):
                    step(b, q)
            for q in range(NQ):
                step(SEQS, q)

        def behind(b):
            return not (isinstance(b, int) and b == 0)

        @block.sync
        def _(sp):
            def load_weights(Q):
                if Q >= 2:
                    sp.wait_ge(s_wl, parts_split(Q - 2, PARTS))
                sp.dma_start(stage[:, Q % 2, :], wprep[Q]).then_inc(s_stage[Q % 2], 16)

            def load_decays(Q):
                sp.dma_start(D[:, Q, :], decay[Q]).then_inc(s_decay[Q % 2], 16)

            sp.dma_start(xs[:, :].rearrange("p (c n) -> p c n", c=NC), xT_t[0]).then_inc(s_xin, 16)
            for i in range(PARTS):
                sp.dma_start(stage[:, 0, i * PART:(i + 1) * PART], wprep[0][:, i * PART:(i + 1) * PART]).then_inc(s_part[i], 16)
            sp.dma_start(nw[:, :], normw).then_inc(s_nwin, 16)
            sp.dma_start(stage[:, 0, PARTS * PART:PREP], wprep[0][:, PARTS * PART:PREP]).then_inc(s_stage[0], 16)
            load_weights(1)
            load_decays(0)
            load_decays(1)
            small = [(ident[:, :], eye), (triu32[:, :], tri), (wr[:, :, :], w_router), (b2[:, :, :], bias2),
                     (wsh[:, :, :], w_shared), (wsd[:, :], w_shared_down), (slotc[:, :], slot_consts)]
            for dst, src in small:
                sp.dma_start(dst, src).then_inc(s_const, 16)
            sp.wait_ge(s_x, 1)
            sp.dma_start(xs[:, :].rearrange("p (c n) -> p c n", c=NC), xT_t[1]).then_inc(s_xin, 16)
            for Q in range(2, NQ):
                load_weights(Q)
                load_decays(Q)
            sp.wait_ge(s_init, 1)
            sp.dma_start(sums[TOK:2 * TOK, :].rearrange("(p k) n -> p (k n)", p=P).rearrange("p (r m) -> p r m", m=HID),
                         zeros[:, :].unsqueeze(1).broadcast_to([P, TOK // P, HID])).then_inc(s_zero, 16)
            for i, opened in enumerate((s_rows, s_base)):
                sp.dma_start(sums[2 * TOK + BAND * i:2 * TOK + BAND * (i + 1), :], zeros[0:BAND, 0:HID]).then_inc(opened, 16)

            def sequence(b):
                if not (isinstance(b, int) and b == SEQS):
                    sp.wait_ge(s_x, b + 1)
                    ahead = (b + 1) % SEQS
                    sp.dma_start(xs[:, :].rearrange("p (c n) -> p c n", c=NC),
                                 xT_t[bass.ds(ahead, 1)].rearrange("o p c n -> (o p) c n")).then_inc(s_xin, 16)
                sp.wait_ge(s_z, b)
                sp.dma_start(xn[:, :, :], x_t[bass.ds(b - 1, 1)].rearrange("o p t n -> (o p) t n")).then_inc(s_xn, 16)
                sp.wait_ge(s_bs, b + 1)
                sp.dma_start(base_t[bass.ds(b - 1, 1)].rearrange("o p t n -> (o p) t n"), bs[:, :, :]).then_inc(s_base, 16)
                sp.wait_ge(s_w, b)
                sp.dma_start(rows_t[bass.ds(b - 1, 1)].rearrange("o p t n -> (o p) t n"), xr[:, :, :]).then_inc(s_rows, 16)

            with sp.Fori(1, SEQS) as b:
                sequence(b)

            def load_pair(p, r):
                one = bass.ds(p, 1)
                sp.dma_start(ring[r][:, 0:4 * NC * FF], w_experts[one].rearrange("o p n -> (o p) n")).then_inc(s_ring[r], 16)
                sp.dma_start(ring[r][0:FF, 4 * NC * FF:PAIR_W], w_down[one].rearrange("o p n -> (o p) n")).then_inc(s_ring[r], 16)

            sp.wait_ge(s_g, STEPS)
            for r in range(RING):
                load_pair(r, r)
            sequence(SEQS)
            with sp.Fori(1, PAIRS // RING) as i:
                for r in range(RING):
                    sp.wait_ge(s_md, RING * (i - 1) + r + 1)
                    load_pair(RING * i + r, r)

            parts = [a.rearrange("(p c k) n -> c p k n", p=P, k=FIN) for a in (sums[0:TOK, :], sums[TOK:2 * TOK, :], out)]
            sp.wait_ge(s_sc, 16 * PAIRS)
            for c in range(FINALS):
                sp.dma_start(f0[c], parts[0][c]).then_inc(s_fl[c], 16)
                sp.dma_start(f1[c], parts[1][c]).then_inc(s_fl[c], 16)
            for c in range(FINALS):
                sp.wait_ge(s_fo, c + 1)
                sp.dma_start(parts[2][c], f1[c]).then_inc(s_out, 16)
            sp.wait_ge(s_out, 16 * FINALS)

        @block.tensor
        def _(pe):
            def group(dst, terms, **kw):
                for i, (a, m) in enumerate(terms):
                    last = nc.tensor.matmul(dst, a, m, start=(i == 0), stop=(i == len(terms) - 1), **kw)
                return last

            PASSES = [(0, 0), (1, 0), (0, 1)]

            def tokens(b, part, c, t0, n):
                at = (b % 2) * (NC * T) + (c * T + t0)
                return (xh, xl)[part][:, bass.ds(at, n)]

            def weights(part, q, col, n):
                return Wv[:, part, q, col:col + n]

            def transposed(b, q, bank, cols):
                for u in range(2):
                    last = group(bank[:, u * T:(u + 1) * T],
                                 [(weights(w, q, cols(c) + u * P, P), tokens(b, t, c, 0, T))
                                  for c in range(NC) for w, t in PASSES])
                return last

            def weights_split(b, q, part):
                if isinstance(b, int) and b == 0:
                    pe.wait_ge(s_wl, parts_split(q, part))

            def project_q(b, q, g):
                weights_split(b, q, 0)
                if q == 0:
                    pe.wait_ge(s_x, b + 1)
                wait(pe, s_qe, g)
                transposed(b, q, pQ, lambda c: c * 256).then_inc(s_q, 1)

            def project_k(b, q, g):
                weights_split(b, q, 1)
                wait(pe, s_ke, g)
                transposed(b, q, pK, lambda c: PART + c * 256).then_inc(s_k, 1)

            def project_v(b, q, g):
                weights_split(b, q, 2)
                wait(pe, s_ve, g)
                for t in range(NT):
                    last = group(pV[:, t * T:(t + 1) * T],
                                 [(tokens(b, tk, c, t * P, P), weights(w, q, 2 * PART + c * 256, QH * HD))
                                  for c in range(NC) for w, tk in PASSES])
                last.then_inc(s_v, 1)

            def project_gate(b, q, g):
                weights_split(b, q, 3)
                wait(pe, s_ge, g)
                transposed(b, q, pG, lambda c: 3 * PART + c * 256).then_inc(s_g, 1)

            def scores(q, h, u):
                if u == 0:
                    pe.wait_ge(s_q2, h + 1)
                    pe.wait_ge(s_k2, h + 1)
                    wait(pe, s_Sm, 2 * h)
                else:
                    pe.wait_ge(s_Sm, 2 * h + 1)
                i = q % 2
                for e in range(2):
                    group(pS0[:, e * T:(e + 1) * T],
                          [(k2[i][:, u, e, 0:P], a[i][:, u, e, :]) for a in (q2h, q2l)])
                    last = group(pS1[:, e * P:(e + 1) * P],
                                 [(k2[i][:, u, e, P:T], a[i][:, u, e, P:T]) for a in (q2h, q2l)])
                last.then_inc(s_S, 1)

            def attention(q, h):
                pe.wait_ge(s_Sm, 2 * h + 2)
                pe.wait_ge(s_ve, h + 1)
                wait(pe, s_sq, h)
                i = q % 2
                for u in range(2):
                    for t in range(NT):
                        for e in range(2):
                            head = 2 * u + e
                            last = nc.tensor.matmul(pC[64 * e:64 * e + 64, u * T + t * P:(u + 1) * T],
                                                    v32[i][:, t, head * HD:(head + 1) * HD],
                                                    S[:, head, 0:T] if t == 0 else S[:, head, T:T + P],
                                                    start=(t == 0), stop=(t == NT - 1))
                last.then_inc(s_C, 1)

            def output(b, q, h):
                pe.wait_ge(s_yl, h + 1)
                if q == 0:
                    wait(pe, s_oe, b)
                for u in range(2):
                    for t in range(NT):
                        for n, (w, y) in enumerate(PASSES):
                            last = nc.tensor.matmul(
                                pO[:, t * HID:(t + 1) * HID], (yh, yl)[y][:, u * T + t * P:u * T + (t + 1) * P],
                                Wo[:, w, q, u * HID:(u + 1) * HID], start=(q == 0 and u == 0 and t == 0 and n == 0),
                                stop=(q == NQ - 1 and u == 1 and n == 2), skip_group_check=True)
                last.then_inc(s_D, 1)

            def piece(b, q, h):
                if q in (1, 2, 3, 4, 5, 6):
                    wait(pe, s_sq, h)
                if q == 1:
                    pe.wait_ge(s_acc, 8 * b)
                    for t in range(NT):
                        last = group(pC[:, t:t + 1], [(acc[:, u * T + t * P:u * T + (t + 1) * P], ones[:, 0:1]) for u in range(2)])
                    last.then_inc(s_ss, 1)
                if q == 2:
                    pe.wait_ge(s_x1, b)
                    for t in range(NT):
                        for c in range(NC):
                            last = nc.tensor.transpose(pC[:, c * T + t * P:c * T + (t + 1) * P],
                                                       xr[:, t, c * P:(c + 1) * P], ident[:, :])
                    last.then_inc(s_T, 1)
                if q == 3:
                    pe.wait_ge(s_x1T, b)
                    for t in range(NT):
                        last = group(pC[:, t * EXP:(t + 1) * EXP],
                                     [(x1T[:, c, t * P:(t + 1) * P], wr[:, c, :]) for c in range(NC)])
                    last.then_inc(s_r, 1)
                if q == 4:
                    pe.wait_ge(s_th, b)
                    for s in range(2):
                        last = group(pC[0:FF, s * T:(s + 1) * T],
                                     [(wsh[:, c, s * FF:(s + 1) * FF], x1T[:, c, :]) for c in range(NC)])
                    last.then_inc(s_gu, 1)
                if q == 5:
                    pe.wait_ge(s_h, b)
                    for t in range(NT):
                        last = group(pC[:, t * HID:(t + 1) * HID], [(hT[:, t * P:(t + 1) * P], wsd[:, :])])
                    last.then_inc(s_dn, 1)
                if q == 6:
                    pe.wait_ge(s_bs, b + 1)
                    pe.wait_ge(s_mask, b)
                    nc.tensor.matmul(pC[0:EXP, 0:T], mask[:, 0, :], triu[:, 0:T], start=True, stop=False)
                    nc.tensor.matmul(pC[0:EXP, P:T], mask[:, 1, :], triu[:, 0:P], start=False, stop=True).then_inc(s_cum, 1)

            def bank_of_attention(b, q):
                if behind(b) and q == 6:
                    pe.wait_ge(s_bs, b + 1)
                elif behind(b) and q >= 2:
                    pe.wait_ge({2: s_sse, 3: s_x1T, 4: s_th, 5: s_h, 7: s_cume}[q], b)

            def step(b, q):
                g = b * NQ + q
                if isinstance(b, int) and b == 0 and q == 2:
                    pe.wait_ge(s_const, 16 * 7)
                    pe.wait_ge(s_tri, 1)
                if isinstance(b, int) and b == SEQS and q >= 2:
                    piece(b, q, STEPS)
                    return
                if has(g):
                    project_q(b, q, g)
                    project_k(b, q, g)
                if has(g - 2):
                    bank_of_attention(b, q)
                    attention((q - 2) % NQ, g - 2)
                if has(g):
                    project_v(b, q, g)
                    project_gate(b, q, g)
                if has(g - 1):
                    scores((q - 1) % NQ, g - 1, 0)
                if has(g - 2):
                    output(b, (q - 2) % NQ, g - 2)
                if has(g - 1):
                    scores((q - 1) % NQ, g - 1, 1)
                if behind(b):
                    piece(b, q, g - 1)

            sequences(pe, step)

            pe.wait_ge(s_ids, 1)
            for dst, a in ((pC, bandg), (pO, bands)):
                last = nc.tensor.matmul(dst[0:BANDS, 0:PAIRS], a[:, :], pairof, start=True, stop=True)
            last.then_inc(s_idp, 1)

            def transpose_rows(p, r):
                pe.wait_ge(s_gath[r], 16 * (p // 4 + 1) if isinstance(p, int) else p * 4 + (16 - 4 * r))
                wait(pe, s_xgT, p - 1)
                for c in range(NC):
                    last = nc.tensor.transpose(pT[r % 2][:, c * P:c * P + BANDS], xg[:, r, c * P:(c + 1) * P],
                                               ident[0:BANDS, 0:BANDS])
                last.then_inc(s_mT, 1)

            def gate_up(p, r):
                pe.wait_ge(s_xgT, p + 1)
                pe.wait_ge(s_ring[r], 32 * (p // 4 + 1) if isinstance(p, int) else p * 8 + (32 - 8 * r))
                wait(pe, s_mh, p - 1)
                for s in range(2):
                    for e in range(2):
                        last = group(pH[r % 2][0:FF, (2 * s + e) * CAP:(2 * s + e + 1) * CAP],
                                     [(ring_gu[r][:, e, s, c, :], xgT[:, r % 2, c, 64 * e:64 * e + CAP]) for c in range(NC)])
                last.then_inc(s_mgu, 1)

            def down(p, r):
                pe.wait_ge(s_mh, p + 1)
                wait(pe, s_wo, p - 1)
                for e in range(2):
                    last = nc.tensor.matmul(pDn[r % 2][64 * e:64 * e + CAP, 0:HID], mh[:, r % 2, e * CAP:(e + 1) * CAP],
                                            ring_d[r][:, e, :], start=True, stop=True)
                last.then_inc(s_md, 1)

            def pairs(i):
                for r in range(RING):
                    p = RING * i + r
                    if not (isinstance(p, int) and p == PAIRS - 1):
                        transpose_rows(p + 1, (r + 1) % RING)
                    gate_up(p, r)
                    if not (isinstance(p, int) and p == 0):
                        down(p - 1, (r - 1) % RING)

            transpose_rows(0, 0)
            pairs(0)
            with pe.Fori(1, PAIRS // RING - 1) as i:
                pairs(i)
            pairs(PAIRS // RING - 1)
            down(PAIRS - 1, RING - 1)

        @block.scalar
        def _(act):
            def split_weights(Q):
                i = Q % 2
                if Q > 0:
                    act.wait_ge(s_stage[i], 16 * (Q // 2 + 1))
                for n, (a, z_) in enumerate(split_ranges(Q)):
                    if Q == 0:
                        act.wait_ge(s_part[n], 16)
                    nc.scalar.activation(Wv[:, 0, Q, a:z_], stage[:, i, a:z_], ACT.Copy, scale=W_SCALE).then_inc(s_wh, 1)
                if Q == 0:
                    act.wait_ge(s_stage[i], 16)
                    act.wait_ge(s_nw, 1)
                for u in range(2):
                    a = QW + GW + u * HID
                    last = nc.scalar.activation(Wo[:, 0, Q, u * HID:(u + 1) * HID], stage[:, i, a:a + HID],
                                                ACT.Copy, scale=nw[:, 2 * Q + u:2 * Q + u + 1])
                last.then_inc(s_wh, 1)

            def act_q(q, g):
                act.wait_ge(s_q, g + 1)
                wait(act, s_q2, g)
                wait(act, s_S, 2 * (g - 1))
                nc.scalar.activation(q32[:, :, :], pQ[:, :].rearrange("p (u n) -> p u n", u=2), ACT.Silu, scale=1 / W_SCALE)
                for e, (a, z_) in enumerate(HALF):
                    src = pQ[a:z_, :].rearrange("p (u n) -> p u n", u=2)
                    for lo, hi in HALF:
                        last = nc.scalar.activation(q2h[q % 2][lo:hi, :, e, :], src, ACT.Silu, scale=1 / W_SCALE)
                last.then_inc(s_qe, 1)

            def act_k(q, g):
                act.wait_ge(s_k, g + 1)
                wait(act, s_k2, g)
                a, b_ = [pK[lo:hi, :].rearrange("p (u n) -> p u n", u=2) for lo, hi in HALF]
                nc.scalar.activation(k32[:, :, :], pK[:, :].rearrange("p (u n) -> p u n", u=2), ACT.Silu, scale=1 / W_SCALE)
                nc.scalar.activation(k2[q % 2][0:64, :, 0, :], a, ACT.Silu, scale=1 / W_SCALE)
                nc.scalar.activation(k2[q % 2][0:64, :, 1, :], b_, ACT.Silu, scale=1 / W_SCALE)
                nc.scalar.activation(khB[64:128, :, :], b_, ACT.Silu, scale=1 / W_SCALE).then_inc(s_ke, 1)

            def act_v(q, g):
                act.wait_ge(s_v, g + 1)
                wait(act, s_C, g - 1)
                nc.scalar.activation(v32[q % 2][:, :, :].rearrange("p t n -> p (t n)"), pV[:, :], ACT.Silu,
                                     scale=1 / W_SCALE).then_inc(s_ve, 1)

            def act_gate(q, g):
                act.wait_ge(s_g, g + 1)
                wait(act, s_y, g - 1)
                nc.scalar.activation(gt[q % 2][:, :], pG[:, :], ACT.Tanh, scale=0.5 / W_SCALE).then_inc(s_ge, 1)

            def act_y(h):
                act.wait_ge(s_y, h + 1)
                wait(act, s_D, h)
                nc.scalar.activation(yh[:, :], y32[:, :], ACT.Copy).then_inc(s_yh, 1)
                wait(act, s_acc, h)
                nc.scalar.activation(sq[:, :], pC[:, :], ACT.Square).then_inc(s_sq, 1)

            def piece(b, q):
                if q == 3:
                    act.wait_ge(s_T, b)
                    nc.scalar.activation(x1T[:, :, :].rearrange("p c n -> p (c n)"), pC[:, :], ACT.Copy).then_inc(s_x1T, 1)
                if q == 4:
                    act.wait_ge(s_r, b)
                    nc.scalar.activation(th[:, :, :].rearrange("p t n -> p (t n)"), pC[:, 0:NT * EXP], ACT.Tanh,
                                         scale=0.5).then_inc(s_th, 1)
                if q == 5:
                    act.wait_ge(s_gu, b)
                    nc.scalar.activation(hs[:, :], pC[0:FF, 0:T], ACT.Silu).then_inc(s_hs, 1)

            def step(b, q):
                g = b * NQ + q
                if behind(b):
                    piece(b, q)
                first = isinstance(b, int) and b == 0
                if first and 0 < q < NQ - 1:
                    split_weights(q + 1)
                if has(g):
                    act_q(q, g)
                if first and q == 0:
                    split_weights(1)
                if has(g - 2):
                    act_y(g - 2)
                if has(g):
                    act_k(q, g)
                    act_v(q, g)
                    act_gate(q, g)

            act.wait_ge(s_xin, 16)
            nc.scalar.activation(xh[:, 0:NC * T], xs[:, :], ACT.Copy).then_inc(s_xh, 1)
            split_weights(0)
            sequences(act, step)

            def evacuate(p, r):
                act.wait_ge(s_mT, p + 1)
                wait(act, s_mgu, p - 1)
                nc.scalar.activation(xgT[:, r % 2, :, :],
                                     pT[r % 2][:, 0:NC * P].rearrange("p (c n) -> p c n", c=NC)[:, :, 0:BANDS],
                                     ACT.Copy).then_inc(s_xgT, 1)

            def pairs(i):
                for r in range(RING):
                    p = RING * i + r
                    if not (isinstance(p, int) and p == PAIRS - 1):
                        evacuate(p + 1, (r + 1) % RING)
                    act.wait_ge(s_mgu, p + 1)
                    wait(act, s_mh, p - 1)
                    nc.scalar.activation(mhs[:, r % 2, :], pH[r % 2][0:FF, 0:2 * CAP], ACT.Silu).then_inc(s_mhs, 1)

            evacuate(0, 0)
            pairs(0)
            with act.Fori(1, PAIRS // RING - 1) as i:
                pairs(i)
            pairs(PAIRS // RING - 1)

            for c in range(FINALS):
                act.wait_ge(s_nm, c + 1)
                for k in range(FIN):
                    last = nc.scalar.activation(f1[c][:, k, :], f0[c][:, k, :], ACT.Identity,
                                                scale=frs[:, c % 2, k:k + 1], bias=nmr[:, c % 2, k:k + 1])
                last.then_inc(s_fo, 1)

        @block.vector
        def _(dve):
            def split_weights(Q):
                i = Q % 2
                for n, (a, z_) in enumerate(split_ranges(Q)):
                    dve.wait_ge(s_wh, parts_split(Q, n))
                    nc.vector.scalar_tensor_tensor(Wv[:, 1, Q, a:z_], stage[:, i, a:z_], W_SCALE, Wv[:, 0, Q, a:z_],
                                                   ALU.mult, ALU.subtract).then_inc(s_wl, 1)
                dve.wait_ge(s_wh, parts_split(Q, PARTS))
                for u in range(2):
                    a = QW + GW + u * HID
                    cols = slice(u * HID, (u + 1) * HID)
                    last = nc.vector.scalar_tensor_tensor(Wo[:, 1, Q, cols], stage[:, i, a:a + HID],
                                                          nw[:, 2 * Q + u:2 * Q + u + 1], Wo[:, 0, Q, cols],
                                                          ALU.mult, ALU.subtract)
                last.then_inc(s_wl, 1)

            def gate(q, h):
                dve.wait_ge(s_C, h + 1)
                dve.wait_ge(s_ge, h + 1)
                nc.vector.scalar_tensor_tensor(y32[:, :], gt[q % 2][:, :], 1.0, pC[:, :], ALU.add, ALU.mult).then_inc(s_y, 1)

            def low_y(h):
                dve.wait_ge(s_yh, h + 1)
                nc.vector.tensor_tensor(yl[:, :], y32[:, :], yh[:, :], ALU.subtract).then_inc(s_yl, 1)

            def low_q(q, g):
                dve.wait_ge(s_qe, g + 1)
                h, l = q2h[q % 2], q2l[q % 2]
                nc.vector.tensor_tensor(l[0:64, :, 0, :], q32[0:64, :, :], h[0:64, :, 0, :], ALU.subtract)
                nc.vector.tensor_tensor(l[64:128, :, 1, :], q32[64:128, :, :], h[64:128, :, 1, :], ALU.subtract).then_inc(s_ql, 1)
                dve.wait_ge(s_ql, g + 1)
                nc.vector.tensor_copy(l[64:128, :, 0, :], l[0:64, :, 0, :])
                nc.vector.tensor_copy(l[0:64, :, 1, :], l[64:128, :, 1, :]).then_inc(s_q2, 1)

            def low_k(q, g):
                dve.wait_ge(s_ke, g + 1)
                k = k2[q % 2]
                nc.vector.tensor_tensor(k[64:128, :, 0, :], k32[0:64, :, :], k[0:64, :, 0, :], ALU.subtract)
                nc.vector.tensor_tensor(k[64:128, :, 1, :], k32[64:128, :, :], khB[64:128, :, :], ALU.subtract).then_inc(s_k2, 1)

            def decayed(b, q, h, u):
                dve.wait_ge(s_S, 2 * h + u + 1)
                if isinstance(b, int) and u == 0 and b == 0:
                    dve.wait_ge(s_decay[q % 2], 16 * (q // 2 + 1))
                d = D[:, q, :].rearrange("p (h n) -> p h n", h=QH)[:, 2 * u:2 * u + 2, :]
                nc.vector.tensor_tensor(S[:, 2 * u:2 * u + 2, 0:T], pS0[:, :].rearrange("p (h n) -> p h n", h=2), d, ALU.mult)
                nc.vector.tensor_tensor(S[:, 2 * u:2 * u + 2, T:T + P], pS1[:, 0:2 * P].rearrange("p (h n) -> p h n", h=2),
                                        d[:, :, 0:P], ALU.mult).then_inc(s_Sm, 1)

            def norm_sums(b):
                f = (2 * W_SCALE) ** 2
                dve.wait_ge(s_ss, b)
                nc.vector.tensor_scalar(ssv[:, :], pC[:, 0:NT], f / INNER, f * EPS, ALU.mult, ALU.add).then_inc(s_sse, 1)

            def residual(b):
                chain = Chain(dve, s_ln1, LN1_LINKS * (b - 1), s_dve_passed)
                dve.wait_ge(s_oe, b)
                dve.wait_ge(s_rstd1, b)
                dve.wait_ge(s_xn, 16 * b)
                for t in range(NT):
                    last = nc.vector.scalar_tensor_tensor(z[:, t, :], o32[:, t, :], rstd1[:, t:t + 1], xn[:, t, :], ALU.mult, ALU.add)
                last.then_inc(s_z, 1)
                dve.wait_ge(s_z, b + 1)
                for t in range(NT):
                    last = nc.vector.bn_stats(st6[:, 0, t, :], z[:, t, :])
                chain.link(last)
                for t in range(NT):
                    last = nc.vector.bn_aggr(mv[:, t, :], st6[:, 0, t, :])
                chain.link(last)
                last = nc.vector.tensor_scalar(vv[:, 0:NT], mv[:, 0:NT, 1], EPS, None, ALU.add)
                chain.link(last)
                nc.vector.tensor_copy(ssv[:, :], vv[:, 0:NT]).then_inc(s_var, 1)
                assert chain.n == LN1_LINKS

            def normed(b):
                dve.wait_ge(s_rstd2, b)
                dve.wait_ge(s_rows, 16 * b)
                for t in range(NT):
                    last = nc.vector.tensor_scalar(xr[:, t, 0:HID], z[:, t, :], mv[:, t, 0:1], rstd2[:, t:t + 1],
                                                   ALU.subtract, ALU.mult)
                last.then_inc(s_x1, 1)

            route = {}

            def route_scores(b):
                chain = route["chain"] = Chain(dve, s_route, ROUTE_LINKS * (b - 1), s_dve_passed)
                dve.wait_ge(s_th, b)
                chain.link(nc.vector.tensor_scalar(sc[:, :, :], th[:, :, :], 0.5, 0.5, ALU.mult, ALU.add))
                chain.link(nc.vector.tensor_tensor(scb[:, :, :], sc[:, :, :], b2[:, :, :], ALU.add))
                by_group = scb[:, :, :].rearrange("p t (g e) -> p (t g) e", g=GROUPS)
                for k in range(NT * GROUPS):
                    last = nc.vector.max(top[:, k, :], by_group[:, k, :])
                chain.link(last)

            def route_groups(b):
                chain = route["chain"]
                best = top[:, :, :].rearrange("p (t g) e -> p t g e", t=NT)
                chain.link(nc.vector.tensor_tensor(gs[:, :, 0:GROUPS], best[:, :, :, 0], best[:, :, :, 1], ALU.add))
                for t in range(NT):
                    last = nc.vector.max(g8[:, t, :], gs[:, t, :])
                chain.link(last)
                chain.link(nc.vector.memset(g8[:, :, TOPG:8], NEG))
                for t in range(NT):
                    last = nc.vector.match_replace(grep[:, t, :], g8[:, t, :], gs[:, t, :], NEG)
                chain.link(last)
                chain.link(nc.vector.tensor_tensor(uns[:, :, :], grep[:, :, 0:GROUPS], gs[:, :, 0:GROUPS], ALU.is_equal))

            def route_experts(b):
                chain = route["chain"]
                out3 = [a[:, :, :].rearrange("p t (g e) -> p (t g) e", g=GROUPS) for a in (masked, scb)]
                dropped = uns[:, :, :].rearrange("p t g -> p (t g)").unsqueeze(2).broadcast_to([P, NT * GROUPS, EXP // GROUPS])
                chain.link(nc.vector.scalar_tensor_tensor(out3[0], dropped, NEG, out3[1], ALU.mult, ALU.add))
                for t in range(NT):
                    last = nc.vector.max(t8[:, t, :], masked[:, t, :])
                chain.link(last)
                chain.link(nc.vector.memset(t8[:, :, TOPK:8], NEG))
                for t in range(NT):
                    last = nc.vector.match_replace(mrep[:, t, :], t8[:, t, :], masked[:, t, :], NEG)
                chain.link(last)
                nc.vector.tensor_tensor(mask[:, :, :], mrep[:, :, :], masked[:, :, :], ALU.not_equal).then_inc(s_mask, 1)

            def route_weights(b):
                chain = route["chain"]
                dve.wait_ge(s_mask, b)
                for t in range(NT):
                    last = nc.vector.scalar_tensor_tensor(wsel[:, t, :], mask[:, t, :], 1.0, sc[:, t, :], ALU.mult, ALU.mult,
                                                          accum_out=wsum[:, t:t + 1])
                chain.link(last)
                chain.link(nc.vector.reciprocal(wrec[:, :], wsum[:, :]))
                for t in range(NT):
                    last = nc.vector.tensor_scalar(xr[:, t, HID:ROW], wsel[:, t, :], wrec[:, t:t + 1], ROUTE_SCALE,
                                                   ALU.mult, ALU.mult)
                last.then_inc(s_w, 1)
                assert chain.n == ROUTE_LINKS, chain.n

            def evacuate_output(b):
                dve.wait_ge(s_D, 8 * b)
                nc.vector.tensor_copy(o32[:, :, :].rearrange("p t n -> p (t n)"), pO[:, :]).then_inc(s_oe, 1)

            def add_shared(b):
                dve.wait_ge(s_dn, b)
                dve.wait_ge(s_base, 16 * b)
                nc.vector.tensor_tensor(bs[:, :, :], pC[:, :].rearrange("p (t n) -> p t n", t=NT), xr[:, :, 0:HID],
                                        ALU.add).then_inc(s_bs, 1)

            def running_counts(b):
                dve.wait_ge(s_cum, b)
                nc.vector.tensor_scalar(cumb[:, 0:T], pC[0:EXP, 0:T], carry[:, 0:1], None, ALU.add).then_inc(s_cume, 1)

            def search(b):
                wait_apart(dve, s_dve_passed, (s_cume, b))
                for k in range(0, CAP, 8):
                    nc.vector.max_index(found[:, k:k + 8], vals[:, k:k + 8], cumb[:, :])

            def fill_slots(b):
                chain = Chain(dve, s_find, FIND_LINKS * (b - 1), s_dve_passed)
                chain.link(nc.vector.tensor_copy(carry[:, :], cumb[:, T - 1:T]))
                chain.link(nc.vector.tensor_copy(foundf[:, :], found[:, :]))
                chain.link(nc.vector.tensor_scalar(pen[:, :], foundf[:, :], float(T), FAR, ALU.is_ge, ALU.mult))
                chain.link(nc.vector.scalar_tensor_tensor(cand[:, :], foundf[:, :], first[:, 0:1], pen[:, :], ALU.add, ALU.add))
                nc.vector.tensor_tensor(ids[:, 0:CAP], ids[:, 0:CAP], cand[:, :], ALU.min)
                chain.link(nc.vector.tensor_scalar(first[:, :], first[:, :], float(T), None, ALU.add))
                assert chain.n == FIND_LINKS, chain.n

            def step(b, q):
                g = b * NQ + q
                if isinstance(b, int) and b == 0 and q == 1:
                    dve.wait_ge(s_const, 16 * 7)
                    nc.vector.tensor_copy(triu[:, :], triu32[:, :]).then_inc(s_tri, 1)
                    dve.wait_ge(s_mhalf, 2)
                    nc.vector.tensor_copy(cumb[:, T:T + CAP], vals[:, :])
                if behind(b):
                    if q == 2:
                        norm_sums(b)
                        evacuate_output(b)
                        residual(b)
                    if q == 4:
                        route_scores(b)
                    if q == 5:
                        dve.wait_ge(s_hs, b)
                        nc.vector.tensor_tensor(hT[:, :], hs[:, :], pC[0:FF, T:2 * T], ALU.mult).then_inc(s_h, 1)
                        route_groups(b)
                    if q == 6:
                        add_shared(b)
                        route_experts(b)
                    if q == 7:
                        running_counts(b)
                        search(b)
                if isinstance(b, int) and b == 0 and q + 1 < NQ:
                    split_weights(q + 1)
                if has(g - 2):
                    gate((q - 2) % NQ, g - 2)
                if has(g):
                    low_q(q, g)
                if has(g - 2):
                    low_y(g - 2)
                if behind(b) and q == 2:
                    normed(b)
                if has(g - 1):
                    decayed(b, (q - 1) % NQ, g - 1, 0)
                if has(g):
                    low_k(q, g)
                if has(g - 1):
                    decayed(b, (q - 1) % NQ, g - 1, 1)
                if isinstance(b, int) and b == 0 and q == NQ - 1:
                    dve.wait_ge(s_decay[q % 2], 16 * (q // 2 + 1))
                if isinstance(b, int) and b == SEQS and q == 1:
                    nc.vector.memset(flat[0:BANDS, 1280:1792], 0.0)
                if behind(b) and q == 7:
                    fill_slots(b)
                    route_weights(b)

            nc.vector.memset(zeros[:, :], 0.0).then_inc(s_init, 1)
            nc.vector.memset(z[:, :, :], 0.0).then_inc(s_z, 1)
            nc.vector.memset(bs[:, :, :], 0.0).then_inc(s_bs, 1)
            for a, value in ((ones[:, :], 1.0), (gs[:, :, :], NEG), (carry[:, :], 0.0), (first[:, :], 0.0),
                             (ids[:, :], 4 * FAR)):
                nc.vector.memset(a, value)
            dve.wait_ge(s_xh, 1)
            nc.vector.tensor_tensor(xl[:, 0:NC * T], xs[:, :], xh[:, 0:NC * T], ALU.subtract).then_inc(s_x, 1)
            dve.wait_ge(s_nwin, 16)
            nc.vector.tensor_scalar(nw[:, :], nw[:, :], W_SCALE, None, ALU.mult).then_inc(s_nw, 1)
            split_weights(0)
            sequences(dve, step)

            chain = Chain(dve, s_slots, 0)
            nc.vector.scalar_tensor_tensor(idss[:, :], ids[:, :], region, dummy, ALU.add, ALU.min)
            chain.link(nc.vector.tensor_scalar(idsg[:, :], ids[:, :], float(TOK - 1), None, ALU.min))
            for dst, src in ((bandg, idsg), (bands, idss)):
                for e, (a, z_) in enumerate(((0, BAND), (BAND, BANDS))):
                    last = nc.vector.tensor_scalar(dst[:, a:z_], src[:, 0:z_ - a], pick[:, e:e + 1], None, ALU.mult)
            last.then_inc(s_ids, 1)
            dve.wait_ge(s_idp, 1)
            nc.vector.tensor_copy(gidx[:, :], pC[0:BANDS, 0:PAIRS])
            nc.vector.tensor_copy(sidx[:, :], pO[0:BANDS, 0:PAIRS]).then_inc(s_idx, 1)
            dve.wait_ge(s_idx, 1)

            def gather_column(p, r):
                nc.vector.tensor_copy(gcol[:, r:r + 1], gidx[:, bass.ds(p, 1)]).then_inc(s_gcol, 1)

            def weigh(p, r):
                dve.wait_ge(s_md, p + 1)
                wait(dve, s_sc, 16 * (p - 1))
                for e in range(2):
                    a = BAND * e
                    last = nc.vector.tensor_scalar(wo[a:a + CAP, r % 2, :], pDn[r % 2][a:a + CAP, 0:HID],
                                                   xg[a:a + CAP, r, bass.ds(2 * p + (HID + e), 1)], None, ALU.mult)
                last.then_inc(s_wo, 1)

            def pairs(i):
                for r in range(RING):
                    p = RING * i + r
                    dve.wait_ge(s_mhs, p + 1)
                    wait(dve, s_md, p - 1)
                    nc.vector.tensor_tensor(mh[:, r % 2, :], mhs[:, r % 2, :], pH[r % 2][0:FF, 2 * CAP:4 * CAP],
                                            ALU.mult).then_inc(s_mh, 1)
                    nc.vector.tensor_copy(scol[:, r:r + 1], sidx[:, bass.ds(p, 1)])
                    if not (isinstance(p, int) and p == 0):
                        weigh(p - 1, (r - 1) % RING)
                    if not (isinstance(p, int) and p + 3 >= PAIRS):
                        gather_column(p + 3, (r + 3) % 4)

            for p in range(3):
                gather_column(p, p)
            pairs(0)
            with dve.Fori(1, PAIRS // RING - 1) as i:
                pairs(i)
            pairs(PAIRS // RING - 1)
            weigh(PAIRS - 1, RING - 1)

            for c in range(FINALS + 2):
                if c < FINALS:
                    dve.wait_ge(s_fl[c], 32)
                    nc.vector.tensor_tensor(f0[c], f0[c], f1[c], ALU.add).then_inc(s_fadd, 1)
                if 1 <= c <= FINALS:
                    dve.wait_ge(s_fst, c)
                    if c >= 3:
                        dve.wait_ge(s_fo, c - 2)
                    for k in range(FIN):
                        last = nc.vector.bn_aggr(fmv[:, (c - 1) % 2, k, :], st6[:, (c - 1) % 2, k, :])
                    last.then_inc(s_fag, 1)
                if c < FINALS:
                    dve.wait_ge(s_fadd, c + 1)
                    for k in range(FIN):
                        last = nc.vector.bn_stats(st6[:, c % 2, k, :], f0[c][:, k, :])
                    last.then_inc(s_fst, 1)
                if 1 <= c <= FINALS:
                    dve.wait_ge(s_fag, c)
                    if c >= 2:
                        dve.wait_ge(s_frs, c - 1)
                    nc.vector.tensor_scalar(vv[:, :], fmv[:, (c - 1) % 2, :, 1], EPS, None, ALU.add).then_inc(s_fv, 1)
                if c >= 2:
                    dve.wait_ge(s_frs, c - 1)
                    nc.vector.scalar_tensor_tensor(nmr[:, c % 2, :], fmv[:, c % 2, :, 0], -1.0, frs[:, c % 2, :],
                                                   ALU.mult, ALU.mult).then_inc(s_nm, 1)

        @block.gpsimd
        def _(pool):
            def split_tokens(b):
                at = (b % 2) * (NC * T)
                waits = [(s_xin, 16 * (b + 1))]
                if not (isinstance(b, int) and b < 2):
                    waits.append((s_g, NQ * (b - 1)))
                wait_apart(pool, s_pool_passed, *waits)
                nc.gpsimd.tensor_copy(xh[:, bass.ds(at, NC * T)], xs[:, :]).then_inc(s_xh, 1)
                pool.wait_ge(s_xh, b + 1)
                nc.gpsimd.tensor_tensor(xl[:, bass.ds(at, NC * T)], xs[:, :], xh[:, bass.ds(at, NC * T)], ALU.subtract).then_inc(s_x, 1)

            def add_squares(b, q, h):
                if q == 0:
                    wait_apart(pool, s_pool_passed, (s_sq, h + 1), (s_ss, b))
                    nc.gpsimd.tensor_copy(acc[:, :], sq[:, :]).then_inc(s_acc, 1)
                else:
                    pool.wait_ge(s_sq, h + 1)
                    pool.wait_ge(s_acc, h)
                    nc.gpsimd.tensor_tensor(acc[:, :], acc[:, :], sq[:, :], ALU.add).then_inc(s_acc, 1)

            def step(b, q):
                g = b * NQ + q
                last_b = isinstance(b, int) and b == SEQS
                if behind(b) and q == 2:
                    pool.wait_ge(s_sse, b)
                    nc.gpsimd.tensor_tensor(rstd1[:, :], ssv[:, :], mhalf[:, 0:NT], ALU.pow).then_inc(s_rstd1, 1)
                    pool.wait_ge(s_var, b)
                    nc.gpsimd.tensor_tensor(rstd2[:, 0:NT], vv[:, 0:NT], mhalf[:, 0:NT], ALU.pow).then_inc(s_rstd2, 1)
                if has(g - 2):
                    add_squares(b, (q - 2) % NQ, g - 2)
                if q == 3 and not last_b:
                    split_tokens(b + 1)

            nc.gpsimd.memset(mhalf[:, :], -0.5).then_inc(s_mhalf, 1)
            nc.gpsimd.iota(vals[:, :], [[1, CAP]], base=1, channel_multiplier=0, allow_small_or_imprecise_dtypes=True).then_inc(s_mhalf, 1)
            sequences(pool, step)

            def gather(p, r):
                wait_apart(pool, s_pool_passed, (s_gcol, p + 1), (s_wo, p - 3))
                nc.gpsimd.indirect_dma_start(xg[:, r, :], None, grows[:, :],
                                             bass.IndirectOffsetOnAxis(ap=gcol[:, r:r + 1], axis=0)).then_inc(s_gath[r], 16)

            def pairs(i):
                for r in range(RING):
                    p = RING * i + r
                    if not (isinstance(p, int) and p + 3 >= PAIRS):
                        gather(p + 3, (r + 3) % 4)
                    wait_apart(pool, s_pool_passed, (s_wo, p + 1), (s_sc, 16 * p))
                    nc.gpsimd.indirect_dma_start(sums[:, :], bass.IndirectOffsetOnAxis(ap=scol[:, r:r + 1], axis=0),
                                                 wo[:, r % 2, :], None, compute_op=ALU.add).then_inc(s_sc, 16)

            pool.wait_ge(s_rows, 16 * (SEQS + 1))
            for p in range(3):
                gather(p, p)
            pool.wait_ge(s_base, 16 * (SEQS + 1))
            pool.wait_ge(s_zero, 16)
            pairs(0)
            with pool.Fori(1, PAIRS // RING - 1) as i:
                pairs(i)
            pairs(PAIRS // RING - 1)

            for c in range(FINALS):
                pool.wait_ge(s_fv, c + 1)
                nc.gpsimd.tensor_tensor(frs[:, c % 2, :], vv[:, :], mhalf[:, :], ALU.pow).then_inc(s_frs, 1)


def kernel(**inputs):
    import numpy as np
    import concourse.bacc as bacc
    from concourse.bass_utils import run_bass_kernel_spmd

    a = {k: np.asarray(v) for k, v in inputs.items()}
    x = np.ascontiguousarray(a["L0_attn_hidden_states"]).reshape(TOK, HID)
    qkv = a["L0_attn_qkv_w"].reshape(NQ, QH, 3, HD, NC, P).transpose(0, 5, 2, 4, 1, 3).reshape(NQ, P, QW)
    gate = a["L0_attn_gate_w"].reshape(NQ, QH * HD, NC, P).transpose(0, 3, 2, 1).reshape(NQ, P, GW)
    wout = a["L0_attn_out_w"].reshape(HID, NQ, 2, P).transpose(1, 3, 2, 0).reshape(NQ, P, OW)
    slope = ((1.0 / 2.0 ** (8.0 / HEADS)) ** (np.arange(HEADS, dtype=np.float32) + np.float32(1.0))).astype(np.float32)
    slope = (slope * np.float32(1.0 - 0 / (32 - 1 + 1e-05) + 1e-05)).astype(np.float32)
    dist = np.arange(T)[None, :] - np.arange(P)[:, None]
    decay = np.where(dist >= 0, np.exp(-slope.astype(np.float64)[:, None, None] * np.maximum(dist, 0)), 0.0).astype(np.float32)
    decay = decay.reshape(NQ, QH, P, T).transpose(0, 2, 1, 3).reshape(NQ, P, QH * T)
    tri = np.concatenate([np.triu(np.ones((P, P), np.float32)), np.ones((P, T - P), np.float32)], axis=1)
    e = np.arange(EXP)
    slot_consts = np.concatenate([e[:, None] % 2 == np.arange(2)[None, :], e[:, None] // 2 == np.arange(PAIRS)[None, :],
                                  TOK * (e[:, None] % 2), 2 * TOK + BAND * (e[:, None] % 2) + np.arange(BAND)[None, :]],
                                 axis=1).astype(np.float32)
    by_chunk = lambda w: w.reshape(NC, P, -1).transpose(1, 0, 2)
    gu = np.stack([a["L0_ffn_w_gate"], a["L0_ffn_w_up"]], axis=1).reshape(PAIRS, 2, 2, NC, P, FF)
    arrays = {
        "x": x,
        "xT": x.T,
        "wprep": np.concatenate([qkv, gate, wout], axis=2),
        "normw": a["L0_attn_norm_w"].reshape(HEADS // 2, P).T,
        "decay": decay,
        "eye": np.eye(P, dtype=np.float32),
        "tri": tri,
        "w_router": by_chunk(a["L0_ffn_gate_w"]),
        "bias2": np.broadcast_to(a["L0_ffn_bias"][None, None, :], (P, NT, EXP)),
        "w_shared": by_chunk(np.concatenate([a["L0_ffn_ws_gate"], a["L0_ffn_ws_up"]], axis=1)),
        "w_shared_down": a["L0_ffn_ws_down"],
        "w_experts": gu.transpose(0, 4, 1, 2, 3, 5).reshape(PAIRS, P, 4 * NC * FF),
        "w_down": a["L0_ffn_w_down"].reshape(PAIRS, 2, FF, HID).transpose(0, 2, 1, 3).reshape(PAIRS, FF, 2 * HID),
        "slot_consts": slot_consts,
    }
    arrays = {k: np.ascontiguousarray(v) for k, v in arrays.items()}
    nc = bacc.Bacc("TRN2", target_bir_lowering=False, num_devices=1)
    aps = {k: nc.dram_tensor(k, v.shape, mybir.dt.from_np(v.dtype), kind="ExternalInput").ap() for k, v in arrays.items()}
    out = nc.dram_tensor("out", (TOK, HID), F32, kind="ExternalOutput").ap()
    block_kernel(nc, **aps, out=out)
    r = run_bass_kernel_spmd(nc, [arrays], core_ids=[0])
    return r.results[0]["out"].reshape(SEQS, T, HID)
```

```python
import concourse.bass as bass
from concourse import mybir
from contextlib import ExitStack

F32 = mybir.dt.float32
F16 = mybir.dt.float16
U32 = mybir.dt.uint32
ALU = mybir.AluOpType
ACT = mybir.ActivationFunctionType

P = 128
SEQS, T, HID = 16, 256, 256
TOK = SEQS * T
HEADS, HD = 32, 64
INNER = HEADS * HD
QH = 4
NQ = HEADS // QH
STEPS = SEQS * NQ
NT = T // P
NC = HID // P
QW, GW, OW = NC * 3 * 256, NC * 256, 2 * HID
PREP = QW + GW + OW
W_SCALE = 1024.0
EPS = 1e-5
EXP, TOPK, GROUPS, TOPG, FF = 64, 6, 8, 4, 96
CAP = 2 * ((2 * 128) * TOPK // EXP)
ROUTE_SCALE = 2.5
PAIRS = EXP // 2
ROW = HID + EXP
BANDS = 112
BAND = 64
NEG = -1e30
FAR = 8192.0
RING = 8
AHEAD = 6
OUTBUF = 4
PAIR_W = 2 * 2 * NC * FF + 2 * HID
FIN = 2
FINALS = TOK // P // FIN
FACT = 4
SH = 256
LN1_LINKS, ROUTE_LINKS, FIND_LINKS = 2, 14, 5


PARTS = 4
PART = NC * 256
EARLY = 3


def split_ranges(quad):
    n = PARTS if quad < EARLY else 2
    return [(i * (PARTS * PART // n), (i + 1) * (PARTS * PART // n)) for i in range(n)]


def parts_split(quad, part):
    before = sum(len(split_ranges(i)) + 1 for i in range(quad))
    return before + part * len(split_ranges(quad)) // PARTS + 1


def wait(eng, sem, value):
    if not (isinstance(value, int) and value <= 0):
        eng.wait_ge(sem, value)


def wait_apart(eng, passed, *waits):
    for sem, v in waits:
        wait(eng, sem, v)
    eng.sem_inc(passed, 1)


class Chain:

    def __init__(self, eng, sem, before, passed=None):
        self.eng, self.sem, self.before, self.n, self.passed = eng, sem, before, 0, passed

    def link(self, instruction):
        self.n += 1
        instruction.then_inc(self.sem, 1)
        if self.passed is None:
            self.eng.wait_ge(self.sem, self.before + self.n)
        else:
            wait_apart(self.eng, self.passed, (self.sem, self.before + self.n))


def block_kernel(nc, x, xT, wprep, normw, decay, eye, tri, w_router, bias2, w_shared, w_shared_down,
                 w_experts, w_down, slot_consts, out):
    grows = nc.dram_tensor("gather_rows", (TOK, ROW), F32, kind="Internal").ap()
    sums = nc.dram_tensor("sums", (2 * TOK + P, HID), F32, kind="Internal").ap()
    x_t = x.rearrange("(b t p) n -> b p t n", t=NT, p=P)
    xT_t = xT.rearrange("(c p) (b n) -> b p c n", p=P, b=SEQS)
    tiles = grows.rearrange("(j p) n -> j p n", p=P)[:, :, 0:HID]
    rows_t = grows.rearrange("(b t p) n -> b p t n", t=NT, p=P)

    with ExitStack() as ctx:
        def sb(name, shape, dt=F32):
            return ctx.enter_context(nc.sbuf_tensor(f"sb_{name}", shape, dt))

        def sem(name):
            return ctx.enter_context(nc.semaphore(name))

        W = sb("W", [P, 2 * NQ * (QW + GW)], F16)
        Wv = W[:, :].rearrange("p (s q n) -> p s q n", s=2, q=NQ)
        Wo = sb("Wo", [P, 2, NQ, OW], F16)
        stage = sb("stage", [P, 2, PREP])
        D = sb("D", [P, NQ, QH * T])
        nw = sb("nw", [P, HEADS // 2])
        xs = sb("xs", [P, NC * T])
        xh = sb("xh", [P, 2 * NC * T], F16)
        xl = sb("xl", [P, 2 * NC * T], F16)
        xn = sb("xn", [P, NT, HID])
        q32 = sb("q32", [P, 2, T])
        k32 = sb("k32", [P, 2, T])
        q2h = [sb(f"q2h{i}", [P, 2, 2, T], F16) for i in range(2)]
        q2l = [sb(f"q2l{i}", [P, 2, 2, T], F16) for i in range(2)]
        k2 = [sb(f"k2{i}", [P, 2, 2, T], F16) for i in range(2)]
        khB = sb("khB", [P, 2, T], F16)
        v32 = [sb(f"v32{i}", [P, NT, QH * HD]) for i in range(2)]
        gt = [sb(f"gt{i}", [P, 2 * T]) for i in range(2)]
        S = sb("S", [P, QH, T + P])
        y32 = sb("y32", [P, 2 * T])
        yh = sb("yh", [P, 2 * T], F16)
        yl = sb("yl", [P, 2 * T], F16)
        sq = sb("sq", [P, 2 * T])
        fold = sb("fold", [P, T])
        acc = sb("acc", [P, T])
        z = sb("z", [P, NT, HID])
        ssv = sb("ssv", [P, NT])
        rstd1 = sb("rstd1", [P, NT])
        mhalf = sb("mhalf", [P, FIN])
        st6 = sb("st6", [P, 2, FIN, 6])
        mv = sb("mv", [P, FIN, 2])
        vv = sb("vv", [P, FIN])
        rstd2 = sb("rstd2", [P, FIN])
        nmr = sb("nmr", [P, FACT, FIN])
        frs = sb("frs", [P, FACT, FIN])
        fmv = sb("fmv", [P, FACT, FIN, 2])
        xr = sb("xr", [P, NT, ROW])
        x1T = sb("x1T", [P, NC, T])
        wr = sb("wr", [P, NC, EXP])
        wsh = sb("wsh", [P, NC, 2 * FF])
        wsd = sb("wsd", [FF, HID])
        b2 = sb("b2", [P, NT, EXP])
        ident = sb("ident", [P, P])
        triu = sb("triu", [P, T], F16)
        triu32 = sb("triu32", [P, T])
        ones = sb("ones", [P, 1])
        th = sb("th", [P, NT, EXP])
        sc = sb("sc", [P, NT, EXP])
        scb = sb("scb", [P, NT, EXP])
        top = sb("top", [P, NT * GROUPS, 8])
        gs = sb("gs", [P, NT, 2 * GROUPS])
        g8 = sb("g8", [P, NT, 8])
        grep = sb("grep", [P, NT, 2 * GROUPS])
        uns = sb("uns", [P, NT, GROUPS])
        masked = sb("masked", [P, NT, EXP])
        t8 = sb("t8", [P, NT, 8])
        mrep = sb("mrep", [P, NT, EXP])
        mask = sb("mask", [P, NT, EXP], F16)
        wsel = sb("wsel", [P, NT, EXP])
        wsum = sb("wsum", [P, NT])
        wrec = sb("wrec", [P, NT])
        cumb = sb("cumb", [EXP, T + CAP])
        carry = sb("carry", [EXP, 1])
        vals = sb("vals", [EXP, CAP])
        found = sb("found", [EXP, CAP], U32)
        foundf = sb("foundf", [EXP, CAP])
        pen = sb("pen", [EXP, CAP])
        cand = sb("cand", [EXP, CAP])
        ids = sb("ids", [EXP, BAND])
        idsg = sb("idsg", [EXP, BAND])
        idss = sb("idss", [EXP, BAND])
        first = sb("first", [EXP, 1])
        slotc = sb("slotc", [EXP, 3 + PAIRS + BAND])
        pick, pairof, region, dummy = (slotc[:, 0:2], slotc[:, 2:2 + PAIRS], slotc[:, 2 + PAIRS:3 + PAIRS],
                                       slotc[:, 3 + PAIRS:3 + PAIRS + BAND])
        bandg = sb("bandg", [EXP, BANDS])
        bands = sb("bands", [EXP, BANDS])
        gidx = sb("gidx", [BANDS, PAIRS], U32)
        sidx = sb("sidx", [BANDS, PAIRS], U32)
        gcol = sb("gcol", [BANDS, RING], U32)
        scol = sb("scol", [BANDS, RING], U32)
        zeros = sb("zeros", [P, HID])
        flat = stage[:, :, :].rearrange("p s n -> p (s n)")
        at = [0]

        def carve(parts, bufs, n):
            at.append(at[-1] + bufs * n)
            return flat[0:parts, at[-2]:at[-1]].rearrange("p (s n) -> p s n", s=bufs)

        xg = carve(BANDS, RING, ROW)
        wo = carve(BANDS, OUTBUF, HID)
        xgT = carve(P, 2, NC * BANDS).rearrange("p s (c n) -> p s c n", c=NC)
        mhs, mh, mhT = carve(BANDS, 2, FF), carve(BANDS, 2, FF), carve(FF, 2, BANDS)
        shs = carve(FF, 2, P)
        W32 = W[:, :].bitcast(F32)
        D1 = D[:, :, :].rearrange("p q n -> p (q n)")
        shared_at = TOK // P * HID
        in_d = NQ * QH * T // PAIR_W
        ring = [D1[:, r * PAIR_W:(r + 1) * PAIR_W] for r in range(in_d)]
        ring += [W32[:, shared_at + r * PAIR_W:shared_at + (r + 1) * PAIR_W] for r in range(RING - in_d)]
        ring_gu = [s[:, 0:4 * NC * FF].rearrange("p (e c n) -> p e c n", e=2, c=NC) for s in ring]
        ring_d = [s[0:FF, 4 * NC * FF:PAIR_W].rearrange("p (e n) -> p e n", e=2) for s in ring]
        CHUNK = FIN * HID
        f0 = [D1[:, c * CHUNK:(c + 1) * CHUNK].rearrange("p (k n) -> p k n", k=FIN) for c in range(FINALS)]
        f1 = [W32[:, shared_at + c * CHUNK:shared_at + (c + 1) * CHUNK].rearrange("p (k n) -> p k n", k=FIN) for c in range(FINALS)]
        shared = W32[:, 0:shared_at].rearrange("p (t n) -> p t n", n=HID)
        fo = [shared[:, c * FIN:(c + 1) * FIN, :] for c in range(FINALS)]
        rest = W32[:, shared_at + (RING - in_d) * PAIR_W:]
        x1s = rest[:, 0:RING * HID].rearrange("p (s n) -> p s n", s=RING)
        a = RING * HID
        sxT = rest[:, a:a + 2 * NC * P].rearrange("p (s c n) -> p s c n", s=2, c=NC)
        a += 2 * NC * P
        sh = rest[0:FF, a:a + OUTBUF * P].rearrange("p (s n) -> p s n", s=OUTBUF)

        pQ, pK, pV, pG, pS0, pS1, pC, pO = [
            ctx.enter_context(nc.psum_tensor(n, [P, 512], F32))
            for n in ("pQ", "pK", "pV", "pG", "pS0", "pS1", "pC", "pO")]
        pT, pH, pHT, pDn = [pQ, pG], [pK, pS0], [pC, pO], [pV, pS1]

        s_dve_passed, s_pool_passed = sem("s_dve_passed"), sem("s_pool_passed")
        s_const = sem("s_const")
        s_init = sem("s_init")
        s_tri = sem("s_tri")
        s_nwin, s_nw = sem("s_nwin"), sem("s_nw")
        s_mhalf = sem("s_mhalf")
        s_part = [sem(f"s_part{i}") for i in range(PARTS)]
        s_stage = [sem(f"s_stage{i}") for i in range(2)]
        s_decay = [sem(f"s_decay{i}") for i in range(NQ)]
        s_wh, s_wl = sem("s_wh"), sem("s_wl")
        s_xin = sem("s_xin")
        s_xh = sem("s_xh")
        s_x = sem("s_x")
        s_xn = sem("s_xn")
        s_q, s_k, s_v, s_g = sem("s_q"), sem("s_k"), sem("s_v"), sem("s_g")
        s_qe, s_ke, s_ve, s_ge = sem("s_qe"), sem("s_ke"), sem("s_ve"), sem("s_ge")
        s_ql = sem("s_ql")
        s_q2 = sem("s_q2")
        s_k2 = sem("s_k2")
        s_S = sem("s_S")
        s_Sm = sem("s_Sm")
        s_C = sem("s_C")
        s_y = sem("s_y")
        s_yh, s_yl = sem("s_yh"), sem("s_yl")
        s_sq = sem("s_sq")
        s_fold, s_acc = sem("s_fold"), sem("s_acc")
        s_D = sem("s_D")
        s_ss, s_sse = sem("s_ss"), sem("s_sse")
        s_rstd1 = sem("s_rstd1")
        s_ln1 = sem("s_ln1")
        s_z = sem("s_z")
        s_var, s_rstd2 = sem("s_var"), sem("s_rstd2")
        s_x1 = sem("s_x1")
        s_T, s_x1T = sem("s_T"), sem("s_x1T")
        s_r, s_th = sem("s_r"), sem("s_th")
        s_route = sem("s_route")
        s_mask, s_w = sem("s_mask"), sem("s_w")
        s_tile = [sem(f"s_tile{i}") for i in range(RING)]
        s_sho = sem("s_sho")
        s_cum, s_cume = sem("s_cum"), sem("s_cume")
        s_find = sem("s_find")
        s_rows = sem("s_rows")
        s_zero = sem("s_zero")
        s_ids, s_idp, s_idx = sem("s_ids"), sem("s_idp"), sem("s_idx")
        s_slots = sem("s_slots")
        s_gcol = sem("s_gcol")
        s_ring = [sem(f"s_ring{i}") for i in range(RING)]
        s_gath = [sem(f"s_gath{i}") for i in range(RING)]
        s_mT, s_xgT = sem("s_mT"), sem("s_xgT")
        s_mgu, s_mhs, s_mh = sem("s_mgu"), sem("s_mhs"), sem("s_mh")
        s_mht, s_mhT = sem("s_mht"), sem("s_mhT")
        s_md, s_wo = sem("s_md"), sem("s_wo")
        s_sc = sem("s_sc")
        s_fl = [sem(f"s_fl{i}") for i in range(FINALS)]
        s_fadd, s_fst, s_fag = sem("s_fadd"), sem("s_fst"), sem("s_fag")
        s_fv, s_frs, s_nm, s_fo, s_out = sem("s_fv"), sem("s_frs"), sem("s_nm"), sem("s_fo"), sem("s_out")

        block = ctx.enter_context(nc.Block())
        HALF = [(0, 64), (64, 128)]

        def has(g):
            return not isinstance(g, int) or 0 <= g < STEPS

        def sequences(eng, step):
            for q in range(NQ):
                step(0, q)
            with eng.Fori(1, SEQS) as b:
                for q in range(NQ):
                    step(b, q)
            for q in range(NQ):
                step(SEQS, q)

        def behind(b):
            return not (isinstance(b, int) and b == 0)

        @block.sync
        def _(sp):
            def load_weights(Q):
                if Q >= 2:
                    sp.wait_ge(s_wl, parts_split(Q - 2, PARTS))
                sp.dma_start(stage[:, Q % 2, :], wprep[Q]).then_inc(s_stage[Q % 2], 16)

            def load_decays(Q):
                sp.dma_start(D[:, Q, :], decay[Q]).then_inc(s_decay[Q], 16)

            sp.dma_start(xs[:, :].rearrange("p (c n) -> p c n", c=NC), xT_t[0]).then_inc(s_xin, 16)
            for i in range(PARTS):
                sp.dma_start(stage[:, 0, i * PART:(i + 1) * PART], wprep[0][:, i * PART:(i + 1) * PART]).then_inc(s_part[i], 16)
            sp.dma_start(nw[:, :], normw).then_inc(s_nwin, 16)
            sp.dma_start(stage[:, 0, PARTS * PART:PREP], wprep[0][:, PARTS * PART:PREP]).then_inc(s_stage[0], 16)
            load_weights(1)
            load_decays(0)
            load_weights(2)
            load_decays(1)
            small = [(ident[:, :], eye), (triu32[:, :], tri), (wr[:, :, :], w_router), (b2[:, :, :], bias2),
                     (wsh[:, :, :], w_shared), (wsd[:, :], w_shared_down), (slotc[:, :], slot_consts)]
            sp.wait_ge(s_x, 1)
            sp.dma_start(xs[:, :].rearrange("p (c n) -> p c n", c=NC), xT_t[1]).then_inc(s_xin, 16)
            load_decays(2)
            for Q in range(3, NQ):
                load_weights(Q)
                load_decays(Q)
                if Q == NQ // 2:
                    for dst, src in small:
                        sp.dma_start(dst, src).then_inc(s_const, 16)
            sp.wait_ge(s_init, 1)
            for i in range(2):
                sp.dma_start(sums[TOK * i:TOK * (i + 1), :].rearrange("(p k) n -> p (k n)", p=P).rearrange("p (r m) -> p r m", m=HID),
                             zeros[:, :].unsqueeze(1).broadcast_to([P, TOK // P, HID])).then_inc(s_zero, 16)
            sp.dma_start(sums[2 * TOK:2 * TOK + P, :], zeros[:, :]).then_inc(s_rows, 16)

            def load_tokens(b):
                sp.wait_ge(s_z, b)
                sp.dma_start(xn[:, :, :], x_t[bass.ds(b - 1, 1)].rearrange("o p t n -> (o p) t n")).then_inc(s_xn, 16)

            def store_rows(b):
                sp.wait_ge(s_w, b)
                sp.dma_start(rows_t[bass.ds(b - 1, 1)].rearrange("o p t n -> (o p) t n"), xr[:, :, :]).then_inc(s_rows, 16)

            with sp.Fori(1, SEQS) as b:
                sp.wait_ge(s_x, b + 1)
                ahead = (b + 1) % SEQS
                sp.dma_start(xs[:, :].rearrange("p (c n) -> p c n", c=NC),
                             xT_t[bass.ds(ahead, 1)].rearrange("o p c n -> (o p) c n")).then_inc(s_xin, 16)
                load_tokens(b)
                store_rows(b)
            load_tokens(SEQS)

            def load_pair(p, r):
                one = bass.ds(p, 1)
                sp.dma_start(ring[r][:, 0:4 * NC * FF], w_experts[one].rearrange("o p n -> (o p) n")).then_inc(s_ring[r], 16)
                sp.dma_start(ring[r][0:FF, 4 * NC * FF:PAIR_W], w_down[one].rearrange("o p n -> (o p) n")).then_inc(s_ring[r], 16)

            def load_tile(j, r):
                sp.dma_start(x1s[:, r, :], tiles[bass.ds(j, 1)].rearrange("o p n -> (o p) n")).then_inc(s_tile[r], 16)

            sp.wait_ge(s_g, STEPS)
            for r in range(in_d, RING):
                load_pair(r, r)
            sp.wait_ge(s_rows, 16 * SEQS)
            for r in range(RING):
                load_tile(r, r)
            sp.wait_ge(s_Sm, 2 * STEPS)
            for r in range(in_d):
                load_pair(r, r)
            store_rows(SEQS)
            sp.wait_ge(s_rows, 16 * (SEQS + 1))
            with sp.Fori(0, PAIRS // RING - 1) as i:
                for r in range(RING):
                    before = RING * i + r
                    sp.wait_ge(s_md, before + 1)
                    load_pair(before + RING, r)
                    sp.wait_ge(s_sho, before + 1)
                    load_tile(before + RING, r)

            parts = [a.rearrange("(c k p) n -> c p k n", p=P, k=FIN) for a in (sums[0:TOK, :], sums[TOK:2 * TOK, :], out)]
            sp.wait_ge(s_sc, 16 * PAIRS)
            sp.wait_ge(s_sho, TOK // P)
            for c in range(FINALS):
                sp.dma_start(f0[c], parts[0][c]).then_inc(s_fl[c], 16)
                sp.dma_start(f1[c], parts[1][c]).then_inc(s_fl[c], 16)
            for c in range(FINALS):
                sp.wait_ge(s_fo, c + 1)
                sp.dma_start(parts[2][c], fo[c]).then_inc(s_out, 16)
            sp.wait_ge(s_out, 16 * FINALS)

        @block.tensor
        def _(pe):
            def group(dst, terms, **kw):
                for i, (a, m) in enumerate(terms):
                    last = nc.tensor.matmul(dst, a, m, start=(i == 0), stop=(i == len(terms) - 1), **kw)
                return last

            PASSES = [(0, 0), (1, 0), (0, 1)]

            def tokens(b, part, c, t0, n):
                at = (b % 2) * (NC * T) + (c * T + t0)
                return (xh, xl)[part][:, bass.ds(at, n)]

            def weights(part, q, col, n):
                return Wv[:, part, q, col:col + n]

            def transposed(b, q, bank, cols):
                for u in range(2):
                    last = group(bank[:, u * T:(u + 1) * T],
                                 [(weights(w, q, cols(c) + u * P, P), tokens(b, t, c, 0, T))
                                  for c in range(NC) for w, t in PASSES])
                return last

            def weights_split(b, q, part):
                if isinstance(b, int) and b == 0:
                    pe.wait_ge(s_wl, parts_split(q, part))

            def project_q(b, q, g):
                weights_split(b, q, 0)
                if q == 0:
                    pe.wait_ge(s_x, b + 1)
                wait(pe, s_qe, g)
                transposed(b, q, pQ, lambda c: c * 256).then_inc(s_q, 1)

            def project_k(b, q, g):
                weights_split(b, q, 1)
                wait(pe, s_ke, g)
                transposed(b, q, pK, lambda c: PART + c * 256).then_inc(s_k, 1)

            def project_v(b, q, g):
                weights_split(b, q, 2)
                wait(pe, s_ve, g)
                for t in range(NT):
                    last = group(pV[:, t * T:(t + 1) * T],
                                 [(tokens(b, tk, c, t * P, P), weights(w, q, 2 * PART + c * 256, QH * HD))
                                  for c in range(NC) for w, tk in PASSES])
                last.then_inc(s_v, 1)

            def project_gate(b, q, g):
                weights_split(b, q, 3)
                wait(pe, s_ge, g)
                transposed(b, q, pG, lambda c: 3 * PART + c * 256).then_inc(s_g, 1)

            def scores(q, h, u):
                if u == 0:
                    pe.wait_ge(s_q2, h + 1)
                    pe.wait_ge(s_k2, h + 1)
                    wait(pe, s_Sm, 2 * h)
                else:
                    pe.wait_ge(s_Sm, 2 * h + 1)
                i = q % 2
                for e in range(2):
                    group(pS0[:, e * T:(e + 1) * T],
                          [(k2[i][:, u, e, 0:P], a[i][:, u, e, :]) for a in (q2h, q2l)])
                    last = group(pS1[:, e * P:(e + 1) * P],
                                 [(k2[i][:, u, e, P:T], a[i][:, u, e, P:T]) for a in (q2h, q2l)])
                last.then_inc(s_S, 1)

            def attention(q, h):
                pe.wait_ge(s_Sm, 2 * h + 2)
                pe.wait_ge(s_ve, h + 1)
                wait(pe, s_sq, h)
                i = q % 2
                for u in range(2):
                    for t in range(NT):
                        for e in range(2):
                            head = 2 * u + e
                            last = nc.tensor.matmul(pC[64 * e:64 * e + 64, u * T + t * P:(u + 1) * T],
                                                    v32[i][:, t, head * HD:(head + 1) * HD],
                                                    S[:, head, 0:T] if t == 0 else S[:, head, T:T + P],
                                                    start=(t == 0), stop=(t == NT - 1))
                last.then_inc(s_C, 1)

            def output(b, q, h):
                pe.wait_ge(s_yl, h + 1)
                if q == 0:
                    pe.wait_ge(s_z, b + 1)
                for u in range(2):
                    for t in range(NT):
                        for n, (w, y) in enumerate(PASSES):
                            last = nc.tensor.matmul(
                                pO[:, t * HID:(t + 1) * HID], (yh, yl)[y][:, u * T + t * P:u * T + (t + 1) * P],
                                Wo[:, w, q, u * HID:(u + 1) * HID], start=(q == 0 and u == 0 and t == 0 and n == 0),
                                stop=(q == NQ - 1 and u == 1 and n == 2), skip_group_check=True)
                last.then_inc(s_D, 1)

            def piece(b, q, h):
                if q in (1, 2, 3, 5):
                    wait(pe, s_sq, h)
                if q == 1:
                    pe.wait_ge(s_acc, 8 * b)
                    for t in range(NT):
                        last = group(pC[:, t:t + 1], [(acc[:, t * P:(t + 1) * P], ones[:, 0:1])])
                    last.then_inc(s_ss, 1)
                if q == 2:
                    pe.wait_ge(s_x1, b)
                    for t in range(NT):
                        for c in range(NC):
                            last = nc.tensor.transpose(pC[:, c * T + t * P:c * T + (t + 1) * P],
                                                       xr[:, t, c * P:(c + 1) * P], ident[:, :])
                    last.then_inc(s_T, 1)
                if q == 3:
                    pe.wait_ge(s_x1T, b)
                    for t in range(NT):
                        last = group(pC[:, t * EXP:(t + 1) * EXP],
                                     [(x1T[:, c, t * P:(t + 1) * P], wr[:, c, :]) for c in range(NC)])
                    last.then_inc(s_r, 1)
                if q == 5:
                    pe.wait_ge(s_mask, b)
                    nc.tensor.matmul(pC[0:EXP, 0:T], mask[:, 0, :], triu[:, 0:T], start=True, stop=False)
                    nc.tensor.matmul(pC[0:EXP, P:T], mask[:, 1, :], triu[:, 0:P], start=False, stop=True).then_inc(s_cum, 1)

            def bank_of_attention(b, q):
                done = {2: s_sse, 3: s_x1T, 4: s_th, 6: s_cume}.get(q)
                if behind(b) and done is not None:
                    pe.wait_ge(done, b)

            def step(b, q):
                g = b * NQ + q
                if isinstance(b, int) and b == SEQS and q >= 2:
                    piece(b, q, STEPS)
                    return
                if has(g):
                    project_q(b, q, g)
                    project_k(b, q, g)
                if has(g - 2):
                    bank_of_attention(b, q)
                    attention((q - 2) % NQ, g - 2)
                if has(g):
                    project_v(b, q, g)
                    project_gate(b, q, g)
                if has(g - 1):
                    scores((q - 1) % NQ, g - 1, 0)
                if has(g - 2):
                    output(b, (q - 2) % NQ, g - 2)
                if has(g - 1):
                    scores((q - 1) % NQ, g - 1, 1)
                if behind(b):
                    piece(b, q, g - 1)
                if isinstance(b, int) and b == 0 and q == NQ - 1:
                    pe.wait_ge(s_const, 16 * 7)
                    pe.wait_ge(s_tri, 1)

            sequences(pe, step)

            pe.wait_ge(s_ids, 1)
            for dst, a in ((pC, bandg), (pO, bands)):
                last = nc.tensor.matmul(dst[0:BANDS, 0:PAIRS], a[:, :], pairof, start=True, stop=True)
            last.then_inc(s_idp, 1)

            def transpose_tokens(p, r):
                pe.wait_ge(s_tile[r], 16 * (p // RING + 1) if isinstance(p, int) else p * 2 + (16 - 2 * r))
                pe.wait_ge(s_gath[r], 16 * (p // RING + 1) if isinstance(p, int) else p * 2 + (16 - 2 * r))
                wait(pe, s_xgT, p - 1)
                for c in range(NC):
                    nc.tensor.transpose(pT[r % 2][:, SH + c * P:SH + (c + 1) * P], x1s[:, r, c * P:(c + 1) * P], ident[:, :])
                for c in range(NC):
                    last = nc.tensor.transpose(pT[r % 2][:, c * P:c * P + BANDS], xg[:, r, c * P:(c + 1) * P],
                                               ident[0:BANDS, 0:BANDS])
                last.then_inc(s_mT, 1)

            def gate_up(p, r):
                pe.wait_ge(s_xgT, p + 1)
                pe.wait_ge(s_ring[r], 32 * (p // RING + 1) if isinstance(p, int) else p * 4 + (32 - 4 * r))
                wait(pe, s_mh, p - 1)
                for c in range(NC):
                    for e in range(2):
                        nc.tensor.matmul(pH[r % 2][BAND * e:BAND * e + CAP, 0:2 * FF], xgT[:, r % 2, c, BAND * e:BAND * e + CAP],
                                         ring_gu[r][:, e, c, :], start=(c == 0), stop=(c == NC - 1))
                for s in range(2):
                    last = group(pH[r % 2][0:FF, SH + s * P:SH + (s + 1) * P],
                                 [(wsh[:, c, s * FF:(s + 1) * FF], sxT[:, r % 2, c, :]) for c in range(NC)])
                last.then_inc(s_mgu, 1)

            def transpose_inner(p, r):
                pe.wait_ge(s_mh, p + 1)
                wait(pe, s_mhT, p - 1)
                nc.tensor.transpose(pHT[r % 2][0:FF, 0:BANDS], mh[:, r % 2, :], ident[0:BANDS, 0:BANDS]).then_inc(s_mht, 1)

            def down(p, r):
                pe.wait_ge(s_mhT, p + 1)
                wait(pe, s_sho, p - 1)
                nc.tensor.matmul(pDn[r % 2][:, SH:SH + HID], sh[:, r % OUTBUF, :], wsd[:, :], start=True, stop=True)
                for e in range(2):
                    last = nc.tensor.matmul(pDn[r % 2][BAND * e:BAND * e + CAP, 0:HID], mhT[:, r % 2, BAND * e:BAND * e + CAP],
                                            ring_d[r][:, e, :], start=True, stop=True)
                last.then_inc(s_md, 1)

            def pairs(i):
                for r in range(RING):
                    p = RING * i + r
                    if not (isinstance(p, int) and p == PAIRS - 1):
                        transpose_tokens(p + 1, (r + 1) % RING)
                    gate_up(p, r)
                    if not (isinstance(p, int) and p < 1):
                        transpose_inner(p - 1, (r - 1) % RING)
                    if not (isinstance(p, int) and p < 2):
                        down(p - 2, (r - 2) % RING)

            pe.wait_ge(s_ke, STEPS)
            pe.wait_ge(s_Sm, 2 * STEPS)
            for bank in pH:
                nc.tensor.matmul(bank[0:BANDS, 0:2 * FF], zeros[:, 0:BANDS], zeros[:, 0:2 * FF], start=True, stop=True)
            transpose_tokens(0, 0)
            pairs(0)
            with pe.Fori(1, PAIRS // RING - 1) as i:
                pairs(i)
            pairs(PAIRS // RING - 1)
            transpose_inner(PAIRS - 1, RING - 1)
            for p in (PAIRS - 2, PAIRS - 1):
                down(p, p % RING)

        @block.scalar
        def _(act):
            def split_weights(Q, parts=range(PARTS + 1)):
                i = Q % 2
                if Q > 0 and 0 in parts:
                    act.wait_ge(s_stage[i], 16 * (Q // 2 + 1))
                for n, (a, z_) in enumerate(split_ranges(Q)):
                    if n not in parts:
                        continue
                    if Q == 0:
                        act.wait_ge(s_part[n], 16)
                    nc.scalar.activation(Wv[:, 0, Q, a:z_], stage[:, i, a:z_], ACT.Copy, scale=W_SCALE).then_inc(s_wh, 1)
                if PARTS not in parts:
                    return
                if Q == 0:
                    act.wait_ge(s_stage[i], 16)
                    act.wait_ge(s_nw, 1)
                for u in range(2):
                    a = QW + GW + u * HID
                    last = nc.scalar.activation(Wo[:, 0, Q, u * HID:(u + 1) * HID], stage[:, i, a:a + HID],
                                                ACT.Copy, scale=nw[:, 2 * Q + u:2 * Q + u + 1])
                last.then_inc(s_wh, 1)

            def act_q(q, g):
                act.wait_ge(s_q, g + 1)
                wait(act, s_q2, g)
                wait(act, s_S, 2 * (g - 1))
                nc.scalar.activation(q32[:, :, :], pQ[:, :].rearrange("p (u n) -> p u n", u=2), ACT.Silu, scale=1 / W_SCALE)
                for e, (a, z_) in enumerate(HALF):
                    src = pQ[a:z_, :].rearrange("p (u n) -> p u n", u=2)
                    for lo, hi in HALF:
                        last = nc.scalar.activation(q2h[q % 2][lo:hi, :, e, :], src, ACT.Silu, scale=1 / W_SCALE)
                last.then_inc(s_qe, 1)

            def act_k(q, g):
                act.wait_ge(s_k, g + 1)
                wait(act, s_k2, g)
                a, b_ = [pK[lo:hi, :].rearrange("p (u n) -> p u n", u=2) for lo, hi in HALF]
                nc.scalar.activation(k32[:, :, :], pK[:, :].rearrange("p (u n) -> p u n", u=2), ACT.Silu, scale=1 / W_SCALE)
                nc.scalar.activation(k2[q % 2][0:64, :, 0, :], a, ACT.Silu, scale=1 / W_SCALE)
                nc.scalar.activation(k2[q % 2][0:64, :, 1, :], b_, ACT.Silu, scale=1 / W_SCALE)
                nc.scalar.activation(khB[64:128, :, :], b_, ACT.Silu, scale=1 / W_SCALE).then_inc(s_ke, 1)

            def act_v(q, g):
                act.wait_ge(s_v, g + 1)
                wait(act, s_C, g - 1)
                nc.scalar.activation(v32[q % 2][:, :, :].rearrange("p t n -> p (t n)"), pV[:, :], ACT.Silu,
                                     scale=1 / W_SCALE).then_inc(s_ve, 1)

            def act_gate(q, g):
                act.wait_ge(s_g, g + 1)
                wait(act, s_y, g - 1)
                nc.scalar.activation(gt[q % 2][:, :], pG[:, :], ACT.Tanh, scale=0.5 / W_SCALE).then_inc(s_ge, 1)

            def act_y(h):
                act.wait_ge(s_y, h + 1)
                wait(act, s_D, h)
                nc.scalar.activation(yh[:, :], y32[:, :], ACT.Copy).then_inc(s_yh, 1)
                wait(act, s_fold, h)
                nc.scalar.activation(sq[:, :], pC[:, :], ACT.Square).then_inc(s_sq, 1)

            def piece(b, q):
                if q == 3:
                    act.wait_ge(s_T, b)
                    nc.scalar.activation(x1T[:, :, :].rearrange("p c n -> p (c n)"), pC[:, :], ACT.Copy).then_inc(s_x1T, 1)
                if q == 4:
                    act.wait_ge(s_r, b)
                    nc.scalar.activation(th[:, :, :].rearrange("p t n -> p (t n)"), pC[:, 0:NT * EXP], ACT.Tanh,
                                         scale=0.5).then_inc(s_th, 1)

            def step(b, q):
                g = b * NQ + q
                if behind(b):
                    piece(b, q)
                early = isinstance(b, int) and b == 0 and q + 1 < EARLY
                if isinstance(b, int) and b == 0 and EARLY <= q + 1 < NQ:
                    split_weights(q + 1)
                if has(g):
                    act_q(q, g)
                if early:
                    split_weights(q + 1, (0, 1))
                if has(g - 2):
                    act_y(g - 2)
                if has(g):
                    act_k(q, g)
                    if early:
                        split_weights(q + 1, (2,))
                    act_v(q, g)
                    if early:
                        split_weights(q + 1, (3, PARTS))
                    act_gate(q, g)

            act.wait_ge(s_xin, 16)
            nc.scalar.activation(xh[:, 0:NC * T], xs[:, :], ACT.Copy).then_inc(s_xh, 1)
            split_weights(0)
            sequences(act, step)

            def evacuate(p, r):
                act.wait_ge(s_mT, p + 1)
                wait(act, s_mgu, p - 1)
                bank = pT[r % 2][:, :].rearrange("p (s c n) -> p s c n", s=2, c=NC)
                nc.scalar.activation(xgT[:, r % 2, :, :], bank[:, 0, :, 0:BANDS], ACT.Copy)
                nc.scalar.activation(sxT[:, r % 2, :, :], bank[:, 1, :, :], ACT.Copy).then_inc(s_xgT, 1)

            def pairs(i):
                for r in range(RING):
                    p = RING * i + r
                    if not (isinstance(p, int) and p == PAIRS - 1):
                        evacuate(p + 1, (r + 1) % RING)
                    act.wait_ge(s_mgu, p + 1)
                    wait(act, s_mh, p - 1)
                    nc.scalar.activation(mhs[:, r % 2, :], pH[r % 2][0:BANDS, 0:FF], ACT.Silu)
                    nc.scalar.activation(shs[:, r % 2, :], pH[r % 2][0:FF, SH:SH + P], ACT.Silu).then_inc(s_mhs, 1)
                    if not (isinstance(p, int) and p < 1):
                        evacuate_inner(p - 1, (r - 1) % RING)

            def evacuate_inner(p, r):
                act.wait_ge(s_mht, p + 1)
                wait(act, s_md, p - 1)
                nc.scalar.activation(mhT[:, r % 2, :], pHT[r % 2][0:FF, 0:BANDS], ACT.Copy).then_inc(s_mhT, 1)

            evacuate(0, 0)
            pairs(0)
            with act.Fori(1, PAIRS // RING - 1) as i:
                pairs(i)
            pairs(PAIRS // RING - 1)
            evacuate_inner(PAIRS - 1, RING - 1)

            for c in range(FINALS):
                act.wait_ge(s_nm, c + 1)
                for k in range(FIN):
                    last = nc.scalar.activation(fo[c][:, k, :], f0[c][:, k, :], ACT.Identity,
                                                scale=frs[:, c % FACT, k:k + 1], bias=nmr[:, c % FACT, k:k + 1])
                last.then_inc(s_fo, 1)

        @block.vector
        def _(dve):
            def split_weights(Q, parts=range(PARTS + 1)):
                i = Q % 2
                for n, (a, z_) in enumerate(split_ranges(Q)):
                    if n not in parts:
                        continue
                    dve.wait_ge(s_wh, parts_split(Q, 0) + n)
                    nc.vector.scalar_tensor_tensor(Wv[:, 1, Q, a:z_], stage[:, i, a:z_], W_SCALE, Wv[:, 0, Q, a:z_],
                                                   ALU.mult, ALU.subtract).then_inc(s_wl, 1)
                if PARTS not in parts:
                    return
                dve.wait_ge(s_wh, parts_split(Q, PARTS))
                for u in range(2):
                    a = QW + GW + u * HID
                    cols = slice(u * HID, (u + 1) * HID)
                    last = nc.vector.scalar_tensor_tensor(Wo[:, 1, Q, cols], stage[:, i, a:a + HID],
                                                          nw[:, 2 * Q + u:2 * Q + u + 1], Wo[:, 0, Q, cols],
                                                          ALU.mult, ALU.subtract)
                last.then_inc(s_wl, 1)

            def gate(q, h):
                dve.wait_ge(s_C, h + 1)
                dve.wait_ge(s_ge, h + 1)
                nc.vector.scalar_tensor_tensor(y32[:, :], gt[q % 2][:, :], 1.0, pC[:, :], ALU.add, ALU.mult).then_inc(s_y, 1)

            def low_y(h):
                dve.wait_ge(s_yh, h + 1)
                nc.vector.tensor_tensor(yl[:, :], y32[:, :], yh[:, :], ALU.subtract).then_inc(s_yl, 1)

            def low_q(q, g):
                dve.wait_ge(s_qe, g + 1)
                h, l = q2h[q % 2], q2l[q % 2]
                nc.vector.tensor_tensor(l[0:64, :, 0, :], q32[0:64, :, :], h[0:64, :, 0, :], ALU.subtract)
                nc.vector.tensor_tensor(l[64:128, :, 1, :], q32[64:128, :, :], h[64:128, :, 1, :], ALU.subtract).then_inc(s_ql, 1)

            def spread_low_q(q, g):
                l = q2l[q % 2]
                dve.wait_ge(s_ql, g + 1)
                nc.vector.tensor_copy(l[64:128, :, 0, :], l[0:64, :, 0, :])
                nc.vector.tensor_copy(l[0:64, :, 1, :], l[64:128, :, 1, :]).then_inc(s_q2, 1)

            def low_k(q, g):
                dve.wait_ge(s_ke, g + 1)
                k = k2[q % 2]
                nc.vector.tensor_tensor(k[64:128, :, 0, :], k32[0:64, :, :], k[0:64, :, 0, :], ALU.subtract)
                nc.vector.tensor_tensor(k[64:128, :, 1, :], k32[64:128, :, :], khB[64:128, :, :], ALU.subtract).then_inc(s_k2, 1)

            def decayed(b, q, h, u):
                dve.wait_ge(s_S, 2 * h + u + 1)
                if isinstance(b, int) and u == 0 and b == 0:
                    dve.wait_ge(s_decay[q], 16)
                d = D[:, q, :].rearrange("p (h n) -> p h n", h=QH)[:, 2 * u:2 * u + 2, :]
                nc.vector.tensor_tensor(S[:, 2 * u:2 * u + 2, 0:T], pS0[:, :].rearrange("p (h n) -> p h n", h=2), d, ALU.mult)
                nc.vector.tensor_tensor(S[:, 2 * u:2 * u + 2, T:T + P], pS1[:, 0:2 * P].rearrange("p (h n) -> p h n", h=2),
                                        d[:, :, 0:P], ALU.mult).then_inc(s_Sm, 1)

            def norm_sums(b):
                f = (2 * W_SCALE) ** 2
                dve.wait_ge(s_ss, b)
                nc.vector.tensor_scalar(ssv[:, :], pC[:, 0:NT], f / INNER, f * EPS, ALU.mult, ALU.add).then_inc(s_sse, 1)

            def residual(b):
                chain = Chain(dve, s_ln1, LN1_LINKS * (b - 1), s_dve_passed)
                dve.wait_ge(s_D, 8 * b)
                dve.wait_ge(s_rstd1, b)
                dve.wait_ge(s_xn, 16 * b)
                for t in range(NT):
                    last = nc.vector.scalar_tensor_tensor(z[:, t, :], pO[:, t * HID:(t + 1) * HID], rstd1[:, t:t + 1], xn[:, t, :], ALU.mult, ALU.add)
                last.then_inc(s_z, 1)
                dve.wait_ge(s_z, b + 1)
                for t in range(NT):
                    last = nc.vector.bn_stats(st6[:, 0, t, :], z[:, t, :])
                chain.link(last)
                for t in range(NT):
                    last = nc.vector.bn_aggr(mv[:, t, :], st6[:, 0, t, :])
                chain.link(last)
                nc.vector.tensor_scalar(vv[:, 0:NT], mv[:, 0:NT, 1], EPS, None, ALU.add).then_inc(s_var, 1)
                assert chain.n == LN1_LINKS

            def normed(b):
                dve.wait_ge(s_rstd2, b)
                dve.wait_ge(s_rows, 16 * b)
                for t in range(NT):
                    last = nc.vector.tensor_scalar(xr[:, t, 0:HID], z[:, t, :], mv[:, t, 0:1], rstd2[:, t:t + 1],
                                                   ALU.subtract, ALU.mult)
                last.then_inc(s_x1, 1)

            route = {}

            def route_scores(b):
                chain = route["chain"] = Chain(dve, s_route, ROUTE_LINKS * (b - 1), s_dve_passed)
                dve.wait_ge(s_th, b)
                chain.link(nc.vector.tensor_scalar(sc[:, :, :], th[:, :, :], 0.5, 0.5, ALU.mult, ALU.add))
                chain.link(nc.vector.tensor_tensor(scb[:, :, :], sc[:, :, :], b2[:, :, :], ALU.add))
                by_group = scb[:, :, :].rearrange("p t (g e) -> p (t g) e", g=GROUPS)
                for k in range(NT * GROUPS):
                    last = nc.vector.max(top[:, k, :], by_group[:, k, :])
                chain.link(last)
                best = top[:, :, :].rearrange("p (t g) e -> p t g e", t=NT)
                chain.link(nc.vector.tensor_tensor(gs[:, :, 0:GROUPS], best[:, :, :, 0], best[:, :, :, 1], ALU.add))

            def route_groups(b):
                chain = route["chain"]
                for t in range(NT):
                    last = nc.vector.max(g8[:, t, :], gs[:, t, :])
                chain.link(last)
                chain.link(nc.vector.memset(g8[:, :, TOPG:8], NEG))
                for t in range(NT):
                    last = nc.vector.match_replace(grep[:, t, :], g8[:, t, :], gs[:, t, :], NEG)
                chain.link(last)
                chain.link(nc.vector.tensor_tensor(uns[:, :, :], grep[:, :, 0:GROUPS], gs[:, :, 0:GROUPS], ALU.is_equal))

            def route_experts(b):
                chain = route["chain"]
                out3 = [a[:, :, :].rearrange("p t (g e) -> p (t g) e", g=GROUPS) for a in (masked, scb)]
                dropped = uns[:, :, :].rearrange("p t g -> p (t g)").unsqueeze(2).broadcast_to([P, NT * GROUPS, EXP // GROUPS])
                chain.link(nc.vector.scalar_tensor_tensor(out3[0], dropped, NEG, out3[1], ALU.mult, ALU.add))
                for t in range(NT):
                    last = nc.vector.max(t8[:, t, :], masked[:, t, :])
                chain.link(last)
                chain.link(nc.vector.memset(t8[:, :, TOPK:8], NEG))
                for t in range(NT):
                    last = nc.vector.match_replace(mrep[:, t, :], t8[:, t, :], masked[:, t, :], NEG)
                chain.link(last)
                nc.vector.tensor_tensor(mask[:, :, :], mrep[:, :, :], masked[:, :, :], ALU.not_equal).then_inc(s_mask, 1)

            def route_weights(b):
                chain = route["chain"]
                dve.wait_ge(s_mask, b)
                for t in range(NT):
                    last = nc.vector.scalar_tensor_tensor(wsel[:, t, :], mask[:, t, :], 1.0, sc[:, t, :], ALU.mult, ALU.mult,
                                                          accum_out=wsum[:, t:t + 1])
                chain.link(last)
                chain.link(nc.vector.reciprocal(wrec[:, :], wsum[:, :]))
                for t in range(NT):
                    last = nc.vector.tensor_scalar(xr[:, t, HID:ROW], wsel[:, t, :], wrec[:, t:t + 1], ROUTE_SCALE,
                                                   ALU.mult, ALU.mult)
                last.then_inc(s_w, 1)
                assert chain.n == ROUTE_LINKS, chain.n

            def running_counts(b):
                dve.wait_ge(s_cum, b)
                nc.vector.tensor_scalar(cumb[:, 0:T], pC[0:EXP, 0:T], carry[:, 0:1], None, ALU.add).then_inc(s_cume, 1)

            def search(b):
                wait_apart(dve, s_dve_passed, (s_cume, b))
                for k in range(0, CAP, 8):
                    nc.vector.max_index(found[:, k:k + 8], vals[:, k:k + 8], cumb[:, :])

            def fill_slots(b):
                chain = Chain(dve, s_find, FIND_LINKS * (b - 1), s_dve_passed)
                chain.link(nc.vector.tensor_copy(carry[:, :], cumb[:, T - 1:T]))
                chain.link(nc.vector.tensor_copy(foundf[:, :], found[:, :]))
                chain.link(nc.vector.tensor_scalar(pen[:, :], foundf[:, :], float(T), FAR, ALU.is_ge, ALU.mult))
                chain.link(nc.vector.scalar_tensor_tensor(cand[:, :], foundf[:, :], first[:, 0:1], pen[:, :], ALU.add, ALU.add))
                nc.vector.tensor_tensor(ids[:, 0:CAP], ids[:, 0:CAP], cand[:, :], ALU.min)
                chain.link(nc.vector.tensor_scalar(first[:, :], first[:, :], float(T), None, ALU.add))
                assert chain.n == FIND_LINKS, chain.n

            def step(b, q):
                g = b * NQ + q
                if isinstance(b, int) and b == 0 and q == NQ - 1:
                    dve.wait_ge(s_const, 16 * 7)
                    nc.vector.tensor_copy(triu[:, :], triu32[:, :]).then_inc(s_tri, 1)
                    dve.wait_ge(s_mhalf, 2)
                    nc.vector.tensor_copy(cumb[:, T:T + CAP], vals[:, :])
                if behind(b):
                    if q == 2:
                        norm_sums(b)
                        residual(b)
                    if q == 4:
                        route_scores(b)
                    if q == 5:
                        route_groups(b)
                        route_experts(b)
                    if q == 6:
                        running_counts(b)
                        search(b)
                    if q == 7:
                        fill_slots(b)
                        route_weights(b)
                early = isinstance(b, int) and b == 0 and q + 1 < EARLY
                if isinstance(b, int) and b == 0 and EARLY <= q + 1 < NQ:
                    split_weights(q + 1)
                if has(g - 2):
                    gate((q - 2) % NQ, g - 2)
                if has(g - 1) and early:
                    decayed(b, (q - 1) % NQ, g - 1, 0)
                if has(g):
                    low_q(q, g)
                if early:
                    split_weights(q + 1, (0, 1))
                if has(g - 2):
                    low_y(g - 2)
                if has(g):
                    spread_low_q(q, g)
                if has(g - 1) and not early:
                    decayed(b, (q - 1) % NQ, g - 1, 0)
                if behind(b) and q == 2:
                    normed(b)
                if early:
                    split_weights(q + 1, (2,))
                if has(g):
                    low_k(q, g)
                if has(g - 1):
                    decayed(b, (q - 1) % NQ, g - 1, 1)
                if early:
                    split_weights(q + 1, (3, PARTS))
                if isinstance(b, int) and b == 0 and q == NQ - 1:
                    dve.wait_ge(s_decay[q], 16)
                if isinstance(b, int) and b == SEQS and q == 1:
                    nc.vector.memset(wo, 0.0)

            nc.vector.memset(zeros[:, :], 0.0).then_inc(s_init, 1)
            nc.vector.memset(z[:, :, :], 0.0).then_inc(s_z, 1)
            for a, value in ((ones[:, :], 1.0), (gs[:, :, :], NEG), (carry[:, :], 0.0), (first[:, :], 0.0),
                             (ids[:, :], 4 * FAR)):
                nc.vector.memset(a, value)
            dve.wait_ge(s_xh, 1)
            nc.vector.tensor_tensor(xl[:, 0:NC * T], xs[:, :], xh[:, 0:NC * T], ALU.subtract).then_inc(s_x, 1)
            split_weights(0, range(PARTS))
            dve.wait_ge(s_nwin, 16)
            nc.vector.tensor_scalar(nw[:, :], nw[:, :], W_SCALE, None, ALU.mult).then_inc(s_nw, 1)
            split_weights(0, (PARTS,))
            sequences(dve, step)

            chain = Chain(dve, s_slots, 0)
            nc.vector.scalar_tensor_tensor(idss[:, :], ids[:, :], region, dummy, ALU.add, ALU.min)
            chain.link(nc.vector.tensor_scalar(idsg[:, :], ids[:, :], float(TOK - 1), None, ALU.min))
            for dst, src in ((bandg, idsg), (bands, idss)):
                for e, (a, z_) in enumerate(((0, BAND), (BAND, BANDS))):
                    last = nc.vector.tensor_scalar(dst[:, a:z_], src[:, 0:z_ - a], pick[:, e:e + 1], None, ALU.mult)
            last.then_inc(s_ids, 1)
            dve.wait_ge(s_idp, 1)
            nc.vector.tensor_copy(gidx[:, :], pC[0:BANDS, 0:PAIRS])
            nc.vector.tensor_copy(sidx[:, :], pO[0:BANDS, 0:PAIRS]).then_inc(s_idx, 1)
            dve.wait_ge(s_idx, 1)

            def gather_column(p, r):
                nc.vector.tensor_copy(gcol[:, r:r + 1], gidx[:, bass.ds(p, 1)]).then_inc(s_gcol, 1)

            def weigh(p, r):
                dve.wait_ge(s_md, p + 1)
                wait(dve, s_sc, 16 * (p + 1 - OUTBUF))
                for e in range(2):
                    a = BAND * e
                    last = nc.vector.tensor_scalar(wo[a:a + CAP, r % OUTBUF, :], pDn[r % 2][a:a + CAP, 0:HID],
                                                   xg[a:a + CAP, r, bass.ds(2 * p + (HID + e), 1)], None, ALU.mult)
                last.then_inc(s_wo, 1)
                nc.vector.tensor_tensor(shared[:, bass.ds(p, 1), :].rearrange("p o n -> p (o n)"), pDn[r % 2][:, SH:SH + HID],
                                        x1s[:, r, :], ALU.add).then_inc(s_sho, 1)

            def pairs(i):
                for r in range(RING):
                    p = RING * i + r
                    dve.wait_ge(s_mhs, p + 1)
                    wait(dve, s_mht, p - 1)
                    wait(dve, s_md, p + 1 - OUTBUF)
                    nc.vector.tensor_tensor(sh[:, r % OUTBUF, :], shs[:, r % 2, :], pH[r % 2][0:FF, SH + P:SH + 2 * P], ALU.mult)
                    nc.vector.tensor_tensor(mh[:, r % 2, :], mhs[:, r % 2, :], pH[r % 2][0:BANDS, FF:2 * FF],
                                            ALU.mult).then_inc(s_mh, 1)
                    nc.vector.tensor_copy(scol[:, r:r + 1], sidx[:, bass.ds(p, 1)])
                    if not (isinstance(p, int) and p < 2):
                        weigh(p - 2, (r - 2) % RING)
                    if not (isinstance(p, int) and p + AHEAD >= PAIRS):
                        gather_column(p + AHEAD, (r + AHEAD) % RING)

            for p in range(AHEAD):
                gather_column(p, p)
            pairs(0)
            with dve.Fori(1, PAIRS // RING - 1) as i:
                pairs(i)
            pairs(PAIRS // RING - 1)
            for p in (PAIRS - 2, PAIRS - 1):
                weigh(p, p % RING)

            for c in range(FINALS + 2):
                if c < FINALS:
                    dve.wait_ge(s_fl[c], 32)
                    nc.vector.tensor_tensor(f0[c], f0[c], f1[c], ALU.add).then_inc(s_fadd, 1)
                if 1 <= c <= FINALS:
                    i = c - 1
                    dve.wait_ge(s_fst, c)
                    if i >= FACT:
                        dve.wait_ge(s_fo, i + 1 - FACT)
                    for k in range(FIN):
                        last = nc.vector.bn_aggr(fmv[:, i % FACT, k, :], st6[:, i % 2, k, :])
                    last.then_inc(s_fag, 1)
                if c < FINALS:
                    dve.wait_ge(s_fadd, 2 * c + 1)
                    nc.vector.tensor_tensor(f0[c], f0[c], fo[c], ALU.add).then_inc(s_fadd, 1)
                if 1 <= c <= FINALS:
                    dve.wait_ge(s_fag, c)
                    if c >= 2:
                        dve.wait_ge(s_frs, c - 1)
                    nc.vector.tensor_scalar(vv[:, :], fmv[:, (c - 1) % FACT, :, 1], EPS, None, ALU.add).then_inc(s_fv, 1)
                if c >= 2:
                    i = (c - 2) % FACT
                    dve.wait_ge(s_frs, c - 1)
                    nc.vector.scalar_tensor_tensor(nmr[:, i, :], fmv[:, i, :, 0], -1.0, frs[:, i, :],
                                                   ALU.mult, ALU.mult).then_inc(s_nm, 1)
                if c < FINALS:
                    dve.wait_ge(s_fadd, 2 * c + 2)
                    for k in range(FIN):
                        last = nc.vector.bn_stats(st6[:, c % 2, k, :], f0[c][:, k, :])
                    last.then_inc(s_fst, 1)

        @block.gpsimd
        def _(pool):
            def split_tokens(b):
                at = (b % 2) * (NC * T)
                waits = [(s_xin, 16 * (b + 1))]
                if not (isinstance(b, int) and b < 2):
                    waits.append((s_g, NQ * (b - 1)))
                wait_apart(pool, s_pool_passed, *waits)
                nc.gpsimd.tensor_copy(xh[:, bass.ds(at, NC * T)], xs[:, :]).then_inc(s_xh, 1)
                pool.wait_ge(s_xh, b + 1)
                nc.gpsimd.tensor_tensor(xl[:, bass.ds(at, NC * T)], xs[:, :], xh[:, bass.ds(at, NC * T)], ALU.subtract).then_inc(s_x, 1)

            def add_squares(b, q, h):
                pool.wait_ge(s_sq, h + 1)
                wait(pool, s_acc, h)
                nc.gpsimd.tensor_tensor(fold[:, :], sq[:, 0:T], sq[:, T:2 * T], ALU.add).then_inc(s_fold, 1)
                if q == 0:
                    wait_apart(pool, s_pool_passed, (s_fold, h + 1), (s_ss, b))
                    nc.gpsimd.tensor_copy(acc[:, :], fold[:, :]).then_inc(s_acc, 1)
                else:
                    pool.wait_ge(s_fold, h + 1)
                    nc.gpsimd.tensor_tensor(acc[:, :], acc[:, :], fold[:, :], ALU.add).then_inc(s_acc, 1)

            def step(b, q):
                g = b * NQ + q
                last_b = isinstance(b, int) and b == SEQS
                if behind(b) and q == 2:
                    pool.wait_ge(s_sse, b)
                    nc.gpsimd.tensor_tensor(rstd1[:, :], ssv[:, :], mhalf[:, 0:NT], ALU.pow).then_inc(s_rstd1, 1)
                    pool.wait_ge(s_var, b)
                    nc.gpsimd.tensor_tensor(rstd2[:, 0:NT], vv[:, 0:NT], mhalf[:, 0:NT], ALU.pow).then_inc(s_rstd2, 1)
                if has(g - 2):
                    add_squares(b, (q - 2) % NQ, g - 2)
                if q == 3 and not last_b:
                    split_tokens(b + 1)

            nc.gpsimd.memset(mhalf[:, :], -0.5).then_inc(s_mhalf, 1)
            nc.gpsimd.iota(vals[:, :], [[1, CAP]], base=1, channel_multiplier=0, allow_small_or_imprecise_dtypes=True).then_inc(s_mhalf, 1)
            sequences(pool, step)

            def gather(p, r):
                wait_apart(pool, s_pool_passed, (s_gcol, p + 1), (s_wo, p + 1 - RING))
                nc.gpsimd.indirect_dma_start(xg[:, r, :], None, grows[:, :],
                                             bass.IndirectOffsetOnAxis(ap=gcol[:, r:r + 1], axis=0)).then_inc(s_gath[r], 16)

            def pairs(i):
                for r in range(RING):
                    p = RING * i + r
                    if not (isinstance(p, int) and p + AHEAD >= PAIRS):
                        gather(p + AHEAD, (r + AHEAD) % RING)
                    wait_apart(pool, s_pool_passed, (s_wo, p + 1), (s_sc, 16 * p))
                    nc.gpsimd.indirect_dma_start(sums[:, :], bass.IndirectOffsetOnAxis(ap=scol[:, r:r + 1], axis=0),
                                                 wo[:, r % OUTBUF, :], None, compute_op=ALU.add).then_inc(s_sc, 16)

            pool.wait_ge(s_rows, 16 * (SEQS + 1))
            for p in range(AHEAD):
                gather(p, p)
            pool.wait_ge(s_zero, 32)
            pairs(0)
            with pool.Fori(1, PAIRS // RING - 1) as i:
                pairs(i)
            pairs(PAIRS // RING - 1)

            for c in range(FINALS):
                pool.wait_ge(s_fv, c + 1)
                nc.gpsimd.tensor_tensor(frs[:, c % FACT, :], vv[:, :], mhalf[:, :], ALU.pow).then_inc(s_frs, 1)


def kernel(**inputs):
    import numpy as np
    import concourse.bacc as bacc
    from concourse.bass_utils import run_bass_kernel_spmd

    a = {k: np.asarray(v) for k, v in inputs.items()}
    x = np.ascontiguousarray(a["L0_attn_hidden_states"]).reshape(TOK, HID)
    qkv = a["L0_attn_qkv_w"].reshape(NQ, QH, 3, HD, NC, P).transpose(0, 5, 2, 4, 1, 3).reshape(NQ, P, QW)
    gate = a["L0_attn_gate_w"].reshape(NQ, QH * HD, NC, P).transpose(0, 3, 2, 1).reshape(NQ, P, GW)
    wout = a["L0_attn_out_w"].reshape(HID, NQ, 2, P).transpose(1, 3, 2, 0).reshape(NQ, P, OW)
    slope = ((1.0 / 2.0 ** (8.0 / HEADS)) ** (np.arange(HEADS, dtype=np.float32) + np.float32(1.0))).astype(np.float32)
    slope = (slope * np.float32(1.0 - 0 / (32 - 1 + 1e-05) + 1e-05)).astype(np.float32)
    dist = np.arange(T)[None, :] - np.arange(P)[:, None]
    decay = np.where(dist >= 0, np.exp(-slope.astype(np.float64)[:, None, None] * np.maximum(dist, 0)), 0.0).astype(np.float32)
    decay = decay.reshape(NQ, QH, P, T).transpose(0, 2, 1, 3).reshape(NQ, P, QH * T)
    tri = np.concatenate([np.triu(np.ones((P, P), np.float32)), np.ones((P, T - P), np.float32)], axis=1)
    e = np.arange(EXP)
    slot_consts = np.concatenate([e[:, None] % 2 == np.arange(2)[None, :], e[:, None] // 2 == np.arange(PAIRS)[None, :],
                                  TOK * (e[:, None] % 2), 2 * TOK + BAND * (e[:, None] % 2) + np.arange(BAND)[None, :]],
                                 axis=1).astype(np.float32)
    by_chunk = lambda w: w.reshape(NC, P, -1).transpose(1, 0, 2)
    gu = np.stack([a["L0_ffn_w_gate"], a["L0_ffn_w_up"]], axis=1).reshape(PAIRS, 2, 2, NC, P, FF)
    arrays = {
        "x": x,
        "xT": x.T,
        "wprep": np.concatenate([qkv, gate, wout], axis=2),
        "normw": a["L0_attn_norm_w"].reshape(HEADS // 2, P).T,
        "decay": decay,
        "eye": np.eye(P, dtype=np.float32),
        "tri": tri,
        "w_router": by_chunk(a["L0_ffn_gate_w"]),
        "bias2": np.broadcast_to(a["L0_ffn_bias"][None, None, :], (P, NT, EXP)),
        "w_shared": by_chunk(np.concatenate([a["L0_ffn_ws_gate"], a["L0_ffn_ws_up"]], axis=1)),
        "w_shared_down": a["L0_ffn_ws_down"],
        "w_experts": gu.transpose(0, 4, 1, 3, 2, 5).reshape(PAIRS, P, 4 * NC * FF),
        "w_down": a["L0_ffn_w_down"].reshape(PAIRS, 2, FF, HID).transpose(0, 2, 1, 3).reshape(PAIRS, FF, 2 * HID),
        "slot_consts": slot_consts,
    }
    arrays = {k: np.ascontiguousarray(v) for k, v in arrays.items()}
    nc = bacc.Bacc("TRN2", target_bir_lowering=False, num_devices=1)
    aps = {k: nc.dram_tensor(k, v.shape, mybir.dt.from_np(v.dtype), kind="ExternalInput").ap() for k, v in arrays.items()}
    out = nc.dram_tensor("out", (TOK, HID), F32, kind="ExternalOutput").ap()
    block_kernel(nc, **aps, out=out)
    r = run_bass_kernel_spmd(nc, [arrays], core_ids=[0])
    return r.results[0]["out"].reshape(SEQS, T, HID)
```
